# Optimizing a Trainium2 kernel written in Bass

```python
import numpy as np
import jax
import jax.numpy as jnp

def _softmax(x, axis=-1):
    return jax.nn.softmax(x, axis=axis)

def _gelu(x):
    return jax.nn.gelu(x, approximate=True)

def _silu(x):
    return jax.nn.silu(x)

def _sigmoid(x):
    return jax.nn.sigmoid(x)

def _layernorm(x, axis=-1, eps=1e-05):
    m = jnp.mean(x, axis=axis, keepdims=True)
    v = jnp.var(x, axis=axis, keepdims=True)
    return (x - m) / jnp.sqrt(v + eps)

def _scatter_add(tgt, idx, src, axis=0):
    return tgt.at[idx].add(src)

def _segment_sum(src, seg, n):
    return jax.ops.segment_sum(src, seg, n)
kernel_name = 'mk_adj_preln_d2_adj_r2_44c9f0'

def setup_inputs(seed: int=0):
    np.random.seed(seed)
    _w = jnp.asarray

    def _rec_inputs():
        import jax
        import jax.numpy as jnp
        _gk = jax.random.key(seed)
        x = 0.0002141 + 1 * jax.random.normal(jax.random.fold_in(_gk, 1), (8192, 64), jnp.float32)
        _a = jax.random.bernoulli(jax.random.fold_in(_gk, 2), 0.000244141, (8192, 8192))
        _af = _a.astype(jnp.float32)
        adj = _af
        return (x, adj)
    x, adj = _rec_inputs()

    def _L0_gnn_setup():
        import jax, jax.numpy as jnp
        import numpy as np
        import math
        N = 6144
        D = 64
        SCALE0 = math.log(10.0)

        def lorentz_linear(x, W, b, scale):
            h = x @ W.T + b
            time = jax.nn.sigmoid(h[:, :1]) * jnp.exp(scale) + 1.1
            xn = h[:, 1:]
            sq = jnp.clip(jnp.sum(xn * xn, axis=-1, keepdims=True), 1e-08, None)
            s = (time * time - 1.0) / sq
            return jnp.concatenate([time, xn * jnp.sqrt(s)], axis=-1)
        key = jax.random.key(seed)
        ks = jax.random.split(key, 8)
        stdv = 1.0 / math.sqrt(D)
        x = jax.random.normal(ks[0], (N, D), dtype=jnp.float32)
        adj = (jax.random.uniform(ks[1], (N, N)) < 0.002).astype(jnp.float32)
        W = jax.random.uniform(ks[2], (D, D), minval=-stdv, maxval=stdv, dtype=jnp.float32)
        Wq = jax.random.uniform(ks[3], (D, D), minval=-stdv, maxval=stdv, dtype=jnp.float32)
        Wk = jax.random.uniform(ks[4], (D, D), minval=-stdv, maxval=stdv, dtype=jnp.float32)
        z = jnp.zeros((D,), dtype=jnp.float32)
        sc = jnp.asarray(SCALE0, dtype=jnp.float32)
        return {'x': x, 'adj': adj, 'W': W, 'b': z, 'scale': sc, 'Wq': Wq, 'bq': z, 'scale_q': sc, 'Wk': Wk, 'bk': z, 'scale_k': sc, 'att_bias': jnp.asarray(20.0, dtype=jnp.float32), 'att_scale': jnp.asarray(math.sqrt(D), dtype=jnp.float32)}
    _L0_gnn_all = _L0_gnn_setup()
    _L0_gnn_in = {k: v for k, v in _L0_gnn_all.items() if k in ('W', 'b', 'scale', 'Wq', 'bq', 'scale_q', 'Wk', 'bk', 'scale_k', 'att_bias', 'att_scale')}
    del _L0_gnn_all

    def _L1_gnn_setup():
        import jax, jax.numpy as jnp
        import numpy as np
        N = 6144
        D_IN = 64
        D_OUT = 64
        BN_EPS = 1e-05
        LEAKY_SLOPE = 0.01

        def _normalize_adj(A):
            n = A.shape[0]
            idx = jnp.arange(n)
            A = A.at[idx, idx].add(1.0)
            d = jax.lax.rsqrt(A.sum(axis=1))
            return d[:, None] * A * d[None, :]
        key = jax.random.key(seed)
        k_h, k_w, k_b, k_a = jax.random.split(key, 4)
        H = jax.random.normal(k_h, (N, D_IN), dtype=jnp.float32)
        W = jax.random.normal(k_w, (D_IN, D_OUT), dtype=jnp.float32) * (1.0 / np.sqrt(D_IN))
        b = jax.random.normal(k_b, (D_OUT,), dtype=jnp.float32) * 0.01
        gamma = jnp.ones((D_OUT,), dtype=jnp.float32)
        beta = jnp.zeros((D_OUT,), dtype=jnp.float32)
        A = jax.random.uniform(k_a, (N, N), dtype=jnp.float32)
        return {'H': H, 'W': W, 'b': b, 'gamma': gamma, 'beta': beta, 'A': A}
    _L1_gnn_all = _L1_gnn_setup()
    _L1_gnn_in = {k: v for k, v in _L1_gnn_all.items() if k in ('W', 'b', 'gamma', 'beta')}
    del _L1_gnn_all
    return {'x': x, 'adj': adj, 'L0_gnn_W': _L0_gnn_in['W'], 'L0_gnn_b': _L0_gnn_in['b'], 'L0_gnn_scale': _L0_gnn_in['scale'], 'L0_gnn_Wq': _L0_gnn_in['Wq'], 'L0_gnn_bq': _L0_gnn_in['bq'], 'L0_gnn_scale_q': _L0_gnn_in['scale_q'], 'L0_gnn_Wk': _L0_gnn_in['Wk'], 'L0_gnn_bk': _L0_gnn_in['bk'], 'L0_gnn_scale_k': _L0_gnn_in['scale_k'], 'L0_gnn_att_bias': _L0_gnn_in['att_bias'], 'L0_gnn_att_scale': _L0_gnn_in['att_scale'], 'L1_gnn_W': _L1_gnn_in['W'], 'L1_gnn_b': _L1_gnn_in['b'], 'L1_gnn_gamma': _L1_gnn_in['gamma'], 'L1_gnn_beta': _L1_gnn_in['beta']}

def reference(x, adj, L0_gnn_W, L0_gnn_b, L0_gnn_scale, L0_gnn_Wq, L0_gnn_bq, L0_gnn_scale_q, L0_gnn_Wk, L0_gnn_bk, L0_gnn_scale_k, L0_gnn_att_bias, L0_gnn_att_scale, L1_gnn_W, L1_gnn_b, L1_gnn_gamma, L1_gnn_beta):
    import jax
    import jax.numpy as jnp

    def _L0_gnn_ref(x, adj, W, b, scale, Wq, bq, scale_q, Wk, bk, scale_k, att_bias, att_scale):
        import jax, jax.numpy as jnp
        import numpy as np
        import math
        N = 6144
        D = 64
        SCALE0 = math.log(10.0)

        def lorentz_linear(x, W, b, scale):
            h = x @ W.T + b
            time = jax.nn.sigmoid(h[:, :1]) * jnp.exp(scale) + 1.1
            xn = h[:, 1:]
            sq = jnp.clip(jnp.sum(xn * xn, axis=-1, keepdims=True), 1e-08, None)
            s = (time * time - 1.0) / sq
            return jnp.concatenate([time, xn * jnp.sqrt(s)], axis=-1)
        h = lorentz_linear(x, W, b, scale)
        q = lorentz_linear(h, Wq, bq, scale_q)
        k = lorentz_linear(h, Wk, bk, scale_k)
        qm = jnp.concatenate([-q[:, :1], q[:, 1:]], axis=-1)
        att = 2.0 + 2.0 * (qm @ k.T)
        att = jax.nn.sigmoid(att / att_scale + att_bias)
        att = adj * att
        support = att @ h
        inner = -support[:, :1] ** 2 + jnp.sum(support[:, 1:] ** 2, axis=-1, keepdims=True)
        denorm = jnp.sqrt(jnp.clip(jnp.abs(-inner), 1e-08, None))
        return support / denorm

    def _L1_gnn_ref(H, W, b, gamma, beta, A):
        import jax, jax.numpy as jnp
        import numpy as np
        N = 6144
        D_IN = 64
        D_OUT = 64
        BN_EPS = 1e-05
        LEAKY_SLOPE = 0.01

        def _normalize_adj(A):
            n = A.shape[0]
            idx = jnp.arange(n)
            A = A.at[idx, idx].add(1.0)
            d = jax.lax.rsqrt(A.sum(axis=1))
            return d[:, None] * A * d[None, :]
        A_hat = _normalize_adj(A)
        X = H @ W + b
        out = A_hat @ X
        mean = out.mean(axis=0)
        var = out.var(axis=0)
        out = (out - mean) * jax.lax.rsqrt(var + BN_EPS) * gamma + beta
        return jax.nn.leaky_relu(out, negative_slope=LEAKY_SLOPE)
    h = jnp.maximum(_layernorm(x, axis=-1), 0.0)
    x = x + _L0_gnn_ref(h, adj, L0_gnn_W, L0_gnn_b, L0_gnn_scale, L0_gnn_Wq, L0_gnn_bq, L0_gnn_scale_q, L0_gnn_Wk, L0_gnn_bk, L0_gnn_scale_k, L0_gnn_att_bias, L0_gnn_att_scale)
    h = jnp.maximum(_layernorm(x, axis=-1), 0.0)
    x = x + _L1_gnn_ref(h, L1_gnn_W, L1_gnn_b, L1_gnn_gamma, L1_gnn_beta, adj)
    return x

_drawn_inputs = setup_inputs


def setup_inputs(seed=0):
    import zlib

    import numpy as np

    out = dict(_drawn_inputs(seed))
    spreads = {'L0_gnn_b': (0.0, 0.1),
     'L0_gnn_bq': (0.0, 2.0),
     'L0_gnn_bk': (0.0, 2.0),
     'L1_gnn_gamma': (1.0, 0.2),
     'L1_gnn_beta': (0.0, 0.1)}
    factors = {'L0_gnn_Wq': 64.0, 'L0_gnn_Wk': 128.137, 'L1_gnn_b': 23.91}
    for name, (base, spread) in spreads.items():
        noise = np.random.default_rng([zlib.crc32(name.encode()), seed]).standard_normal(out[name].shape)
        drawn = base * np.exp(spread * noise) if base else spread * noise
        out[name] = jnp.asarray(drawn.astype(out[name].dtype))
    for name, factor in factors.items():
        out[name] = (out[name] * factor).astype(out[name].dtype)
    return out
```

```python
from contextlib import ExitStack, contextmanager

import concourse.bass as bass
from concourse import mybir

P = 128
ALU = mybir.AluOpType
ACT = mybir.ActivationFunctionType
AX = mybir.AxisListType
F32 = mybir.dt.float32
BF16 = mybir.dt.bfloat16
I32 = mybir.dt.int32
U32 = mybir.dt.uint32

GR = 16
SEC = 1024
SUB = 128
SUBBITS = 7
NSUB = SEC // SUB
SLOTS = 64
RING = 8
EB = 4
PB = 8
TB = 2
CT = 8
LN_EPS = 1e-5
BN_EPS = 1e-5
SLOPE = 0.01


class Count:

    def __init__(self, sem):
        self.sem, self.done, self.off = sem, 0, 0

    def inc(self, ins, by=1):
        ins.then_inc(self.sem, by)
        self.done += by

    def now(self):
        return self.off + self.done

    @contextmanager
    def loop(self, i, trips, per):
        outer, start = self.off, self.done
        self.off = outer + i * per
        yield
        assert self.done - start == per, (self.done - start, per)
        self.off, self.done = outer, start + trips * per


def host_constants(n):
    import numpy as np

    f = np.zeros((P, P + P + 2 * SLOTS), np.float32)
    f[:, 0:P] = np.eye(P)
    f[:, P:2 * P] = 1.0
    for c in range(SLOTS):
        f[2 * c, 2 * P + c] = 1.0
        f[2 * c + 1, 2 * P + SLOTS + c] = 1.0
    b = np.zeros((P, 248 + P + SEC), np.float32)
    for p in range(P):
        b[p, 120 + p // GR] = 2.0 ** (p % GR + SUBBITS)
    b[0, 248:248 + P] = 1.0
    b[0, 248 + P:] = np.arange(SEC) % SUB
    i = np.zeros((P, 2 * GR), np.int32)
    for p in range(P):
        h = p // SLOTS
        i[p, h * GR:(h + 1) * GR] = 2 ** np.arange(GR)
    halves = np.ascontiguousarray(b.view(np.uint16)[:, 1::2])
    return {"const_f": f, "const_b": halves, "const_i": i}


def graph_layers(nc, x, adj, W0, b0, scale0, Wq, bq, scale_q, Wk, bk, scale_k, att_bias, att_scale,
                 W1, b1, gamma, beta, const_f, const_b, const_i, out):
    N, D = x.shape
    NT = N // P
    ST = NT // 16
    NS = N // SEC
    SECT = ST * NS
    BPS = 16 // TB
    NB = ST * BPS
    PAIRS = 64
    NC = NT // CT
    assert NS == BPS == NC == 8 and D == 64

    table = nc.dram_tensor("key_and_h_table", [N, 2 * D], F32).ap()
    ytable = nc.dram_tensor("y_table", [N, D], F32).ap()
    table_t = table.rearrange("(t p) d -> p t d", p=P)
    ytable_t = ytable.rearrange("(t p) d -> p t d", p=P)
    adj_t = adj.rearrange("(t p) n -> t p n", p=P)
    x_t = x.rearrange("(t p) d -> p t d", p=P)
    out_t = out.rearrange("(t p) d -> p t d", p=P)

    with ExitStack() as ctx:
        def sb(name, shape, dt=F32):
            return ctx.enter_context(nc.sbuf_tensor(name, shape, dt))

        def sem(name):
            return ctx.enter_context(nc.semaphore(name))

        xs = sb("x_rows", [P, NT, D])
        agg = sb("aggregated", [P, NT, D])
        ys = sb("y_rows", [P, NT, D])
        deg = sb("degree", [P, NT])
        dinv = sb("inv_sqrt_degree", [P, NT])
        qT = sb("q_transposed", [D, N])
        mask = sb("slot_mask", [P, ST * PAIRS * 32], BF16)
        columns = sb("slot_columns", [P, ST * PAIRS], I32)
        ring = sb("adj_ring", [P, RING, SEC])
        eqb = sb("adj_is_one", [P, EB, SEC], BF16)
        sgb = sb("adj_sign", [P, EB, SEC], BF16)
        differ = sb("packs_differ", [P, SEC])
        best = sb("best_of_subsections", [P, 2, NSUB * 8])
        cand = sb("candidates", [P, NS * NSUB * 8])
        key8 = sb("slot_keys", [P, SLOTS])
        pos8 = sb("slot_positions", [P, SLOTS], U32)
        keyi = sb("slot_keys_int", [P, SLOTS], I32)
        lowi = sb("column_in_subsection", [P, SLOTS], I32)
        colpad = sb("columns_padded", [P, 3 * SLOTS])
        bitpad = sb("bits_padded", [P, 3 * SLOTS])
        biti = sb("slot_bits", [P, PAIRS], I32)
        over = sb("overflow", [P, 2 * ST])
        mis = sb("mismatch", [P, 2])
        misrun = sb("mismatch_any", [P, 1])
        bad = sb("bad", [P, 4])
        flag = sb("flag", [1, 1], I32)
        gat = sb("gathered", [P, 2, PB, 2 * D])
        ygat = gat[:, :, :, 0:D]
        att = sb("attention", [P, PB * 32])
        mstat = sb("batch_mask", [P, 2, PB * 32])
        attm = sb("attention_masked", [P, PB * 32])
        nat = sb("chunk_rows", [P, CT, D])
        hid = sb("chunk_hidden", [P, 2 * CT, D])
        sqr = differ[:].rearrange("p (t d) -> p t d", d=D)
        turned = sb("chunk_transposed", [D + 1, CT * P])
        keyT = turned[0:D, :]
        pnat = sb("batch_rows", [P, TB, D])
        psq = sb("batch_squares", [P, TB, D])
        pxc = sb("batch_centred", [P, TB, D])
        pturned = sb("batch_transposed", [D + 1, TB * P])
        pst = sb("batch_stats", [P, 6, 2 * TB])
        kh = sb("chunk_keys_and_h", [P, CT, 2 * D])
        st = sb("chunk_stats", [P, 8, 2 * CT])
        w0a = sb("w0_aug", [D + 1, D])
        wqk = sb("wqk_aug", [D + 1, 2 * D])
        w1a = sb("w1_aug", [D + 1, D])
        wnat = sb("w_natural", [D, 3, D])
        cf = sb("const_f_sb", [P, 2 * P + 2 * SLOTS])
        cb = sb("const_b_sb", [P, 248 + P + SEC], BF16)
        ci = sb("const_i_sb", [P, 2 * GR], I32)
        NPAR = 5 + 2 * D
        prow = sb("param_row", [1, NPAR])
        par = sb("params", [P, NPAR])
        esc = sb("exp_scales", [P, 3])
        esc_h = sb("exp_scale_h", [P, CT])
        esc_qk = sb("exp_scale_qk", [P, CT, 2])
        att_s = sb("att_scale_bias", [P, 4])
        bn = sb("bn_vectors", [P, 6, D])
        lneps = sb("ln_eps", [P, 1])

        key_ps = [ctx.enter_context(nc.psum_tensor(f"packed_ones_{i}", [P, SEC], F32)) for i in range(2)]
        sign_ps = ctx.enter_context(nc.psum_tensor("packed_signs", [P, SEC], F32))
        work = ctx.enter_context(nc.psum_tensor("work", [P, 1024], F32))

        ident = cf[:, 0:P]
        ones = cf[:, P:2 * P]
        sel_even = cf[:, 2 * P:2 * P + SLOTS]
        sel_odd = cf[:, 2 * P + SLOTS:2 * P + 2 * SLOTS]
        ones_row = cb[:, 248:248 + P]
        column_row = cb[:, 248 + P:248 + P + SEC]

        consts_in = sem("consts_in")
        x_in = sem("x_in")
        adj_in = [sem(f"adj_in_{i}") for i in range(RING)]
        eq_ready = sem("eq_ready")
        sign_ready = sem("sign_ready")
        packed = sem("packed")
        section_read = sem("section_read")
        weights_T = sem("weights_T")
        params_bc = sem("params_broadcast")
        exps_ready = sem("exps_ready")
        setup_done = sem("setup_done")
        dve_step = sem("dve_step")
        names = ("var_ready", "std_ready", "nat_ready", "nat_turned", "nat_copied", "hidden_ready",
                 "gate_ready", "ratio_ready", "root_ready", "h_ready", "h_turned", "h_copied", "qk_ready",
                 "qk_gate_ready", "qk_ratio_ready", "qk_root_ready", "q_ready", "q_turned", "q_copied",
                 "table_written", "slots_ready", "hidden_copied", "qk_copied", "slots_turned", "columns_ready", 
                 "keys_turned", "keys_copied", "scores_ready", "att_ready", "attm_ready",
                 "support_ready", "support_copied", "norm_ready", "norm_root", "x1_var", "x1_std", "x1_nat",
                 "x1_turned", "x1_copied", "xw_ready", "y_ready", "y_written", "signs_copied", "bad_ready", "flag_summed",
                 "flag_ready")
        S = {k: sem(k) for k in names}
        gathered = [sem(f"gathered_{i}") for i in range(2)]

        def over_sections(eng, section, counters=()):
            @contextmanager
            def counted(i, trips, column):
                with ExitStack() as s:
                    for c, *per in counters:
                        s.enter_context(c.loop(i, trips, per[column]))
                    yield
            section(0, 0, 0, 0, first=True)
            section(1, 0, 1, 1)
            with eng.Fori(0, NS // 2 - 1) as k:
                with counted(k, NS // 2 - 1, 0):
                    for odd in range(2):
                        section(2 * k + 2 + odd, 0, 2 * k + 2 + odd, odd)
            for t in range(1, ST):
                for odd in range(2):
                    section(NS * t + odd, t, odd, odd, later=True, compact=(t - 1 if odd == 0 else None))
                with eng.Fori(0, NS // 2 - 1) as k:
                    with counted(k, NS // 2 - 1, 1):
                        for odd in range(2):
                            section(2 * k + NS * t + 2 + odd, t, 2 * k + 2 + odd, odd, later=True)

        def reduce_x(dst, src, op=ALU.add):
            return nc.vector.tensor_reduce(dst, src, AX.X, op)

        def bc(col, g):
            return col.unsqueeze(2).to_broadcast([P, g, D])

        V = nc.vector
        step = Count(dve_step)

        def then(ins, count=step):
            count.inc(ins)
            nc.vector.wait_ge(count.sem, count.now())

        def turn(pe, src, c, ready, done, count=CT):
            if ready:
                pe.wait_ge(S[ready], c + 1)
            for t in range(count):
                if t == 0:
                    pe.matmul(work[0:D, 0:P], src(t), ident, start=True, stop=True)
                    continue
                ins = pe.transpose(work[0:D, t * P:(t + 1) * P], src(t), ident)
            ins.then_inc(S[done], 1)

        def pe_batch(pe, i, b, odd):
            if i == 4:
                pe.wait_ge(gathered[odd], (b - odd) * (8 * PB) + 16 * PB)
                pe.wait_ge(S["y_ready"], b)
                turn(pe, lambda t: gat[:, odd, t, 0:D], b, None, "keys_turned")
            if i == 5:
                pe.wait_ge(S["keys_copied"], b + 1)
                for t in range(PB):
                    ins = pe.matmul(work[:, t * 32:(t + 1) * 32], keyT[:, t * P:(t + 1) * P],
                                    qT[:, bass.ds(b * (PB * 32) + t * 32, 32)], start=True, stop=True)
                ins.then_inc(S["scores_ready"], 1)
            if i == 7:
                pe.wait_ge(S["attm_ready"], b + 1)
                for t in range(PB):
                    q, r = 32 * (t % 4), t // 4
                    pe.matmul(work[q:q + 32, 512 + r * D:512 + (r + 1) * D], attm[:, t * 32:(t + 1) * 32],
                              gat[:, odd, t, D:2 * D], start=True, stop=True, tile_position=(0, q))
                    ins = pe.matmul(work[q:q + 32, 512 + TB * D + r:512 + TB * D + r + 1],
                                    mstat[:, 0, t * 32:(t + 1) * 32], ones[:, 0:1],
                                    start=True, stop=True, tile_position=(0, q))
                ins.then_inc(S["support_ready"], 1)
            pe_post(pe, i, b)

        def act_batch(act, i, b):
            if i == 5:
                act.wait_ge(S["keys_turned"], b + 1)
                act.activation(keyT[:], work[0:D, :], ACT.Copy).then_inc(S["keys_copied"], 1)
            if i == 6:
                act.wait_ge(S["scores_ready"], b + 1)
                act.activation(att[:], work[:, 0:PB * 32], ACT.Sigmoid, bias=att_s[:, 1:2],
                               scale=att_s[:, 0:1]).then_inc(S["att_ready"], 1)
            act_post(act, i, b, b)

        def dve_batch(dve, i, b):
            if i == 5:
                then(V.tensor_copy(mstat[:, 0, :], mask[:, bass.ds(b * (PB * 32), PB * 32)]))
            if i == 6:
                dve.wait_ge(S["att_ready"], b + 1)
                V.tensor_tensor(attm[:], att[:], mstat[:, 0, :], ALU.mult)\
                    .then_inc(S["attm_ready"], 1)
            if i == 8:
                dve.wait_ge(S["support_ready"], b + 1)
                V.tensor_copy(deg[:, bass.ds(b * TB, TB)], work[:, 512 + TB * D:512 + TB * D + TB])
                then(V.tensor_copy(agg[:, bass.ds(b * TB, TB), :],
                                   work[:, 512:512 + TB * D].rearrange("p (t d) -> p t d", d=D)))
            dve_post(dve, i, b, b)

        def pe_post(pe, i, m):
            if i == 12:
                turn(pe, lambda t: pnat[:, t, :], m, "x1_nat", "x1_turned", TB)
            if i == 14:
                pe.wait_ge(S["x1_copied"], m + 1)
                for t in range(TB):
                    ins = pe.matmul(work[:, t * D:(t + 1) * D], pturned[:, t * P:(t + 1) * P], w1a[:],
                                    start=True, stop=True)
                ins.then_inc(S["xw_ready"], 1)

        def act_post(act, i, b, m):
            if i == 9:
                act.wait_ge(S["norm_ready"], m + 1)
                act.activation(pst[:, 1, :], pst[:, 0, :], ACT.Sqrt).then_inc(S["norm_root"], 1)
            if i == 11:
                act.wait_ge(S["x1_var"], m + 1)
                act.activation(pst[:, 3, 0:TB], pst[:, 2, 0:TB], ACT.Sqrt, bias=lneps[:, 0:1])\
                    .then_inc(S["x1_std"], 1)
            if i == 13:
                act.wait_ge(S["x1_turned"], m + 1)
                act.activation(pturned[0:D, :], work[0:D, 0:TB * P], ACT.Copy).then_inc(S["x1_copied"], 1)
            if i == 15:
                act.wait_ge(S["y_ready"], m + 1)
                act.dma_start(ytable_t[:, bass.ds(b * TB, TB), :], ys[:, bass.ds(b * TB, TB), :])\
                    .then_inc(S["y_written"], 16)

        def dve_post(dve, i, b, m, count=step):
            link = lambda ins: then(ins, count)
            rows, cols = bass.ds(b * TB, TB), bass.ds(b * TB, TB)
            if i == 8:
                link(V.tensor_tensor(psq[:], agg[:, rows, :], agg[:, rows, :], ALU.mult))
                V.tensor_scalar(pst[:, 0, TB:2 * TB], deg[:, cols], 1.0, None, ALU.add)
                link(reduce_x(pst[:, 4, 0:TB], psq[:, :, 1:D]))
                link(V.tensor_tensor(pst[:, 4, TB:2 * TB], pst[:, 4, 0:TB], psq[:, :, 0], ALU.subtract))
                link(V.scalar_tensor_tensor(out=pst[:, 4, 0:TB], in0=pst[:, 4, TB:2 * TB], scalar=-1.0,
                                            in1=pst[:, 4, TB:2 * TB], op0=ALU.mult, op1=ALU.max))
                V.tensor_scalar(pst[:, 0, 0:TB], pst[:, 4, 0:TB], 1e-8, None, ALU.max)\
                    .then_inc(S["norm_ready"], 1)
            if i == 10:
                dve.wait_ge(S["norm_root"], m + 1)
                link(V.reciprocal(pst[:, 4, :], pst[:, 1, :]))
                V.tensor_copy(dinv[:, cols], pst[:, 4, TB:2 * TB])
                link(V.tensor_tensor(pxc[:], agg[:, rows, :], bc(pst[:, 4, 0:TB], TB), ALU.mult))
                link(V.tensor_tensor(psq[:], xs[:, rows, :], pxc[:], ALU.add))
                reduce_x(pst[:, 5, 0:TB], psq[:])
                link(V.tensor_copy(xs[:, rows, :], psq[:]))
                link(V.tensor_scalar(pst[:, 5, 0:TB], pst[:, 5, 0:TB], 1.0 / D, None, ALU.mult))
                link(V.tensor_tensor(pxc[:], psq[:], bc(pst[:, 5, 0:TB], TB), ALU.subtract))
                link(V.tensor_tensor(psq[:], pxc[:], pxc[:], ALU.mult))
                link(reduce_x(pst[:, 5, TB:2 * TB], psq[:]))
                V.tensor_scalar(pst[:, 2, 0:TB], pst[:, 5, TB:2 * TB], 1.0 / D, None, ALU.mult)\
                    .then_inc(S["x1_var"], 1)
            if i == 12:
                dve.wait_ge(S["x1_std"], m + 1)
                link(V.reciprocal(pst[:, 5, 0:TB], pst[:, 3, 0:TB]))
                link(V.tensor_tensor(psq[:], pxc[:], bc(pst[:, 5, 0:TB], TB), ALU.mult))
                V.tensor_scalar(pnat[:], psq[:], 0.0, None, ALU.max).then_inc(S["x1_nat"], 1)
            if i == 15:
                dve.wait_ge(S["xw_ready"], m + 1)
                V.tensor_tensor(ys[:, rows, :], work[:, 0:TB * D].rearrange("p (t d) -> p t d", d=D),
                                bc(dinv[:, cols], TB), ALU.mult).then_inc(S["y_ready"], 1)

        with nc.Block() as block:
            @block.sync
            def _(sp):
                for dst, src in ((cf[:], const_f), (cb[:], const_b.bitcast(BF16)), (ci[:], const_i),
                                 (wnat[:, 0, :], W0), (wnat[:, 1, :], Wq), (wnat[:, 2, :], Wk),
                                 (w1a[0:D, :], W1),
                                 (w0a[D:D + 1, :], b0.rearrange("(a d) -> a d", a=1)),
                                 (wqk[D:D + 1, 0:D], bq.rearrange("(a d) -> a d", a=1)),
                                 (wqk[D:D + 1, D:2 * D], bk.rearrange("(a d) -> a d", a=1)),
                                 (w1a[D:D + 1, :], b1.rearrange("(a d) -> a d", a=1)),
                                 (prow[0:1, 5:5 + D], gamma.rearrange("(a d) -> a d", a=1)),
                                 (prow[0:1, 5 + D:5 + 2 * D], beta.rearrange("(a d) -> a d", a=1))):
                    sp.dma_start(dst, src).then_inc(consts_in, 16)
                for j, s in enumerate((scale0, scale_q, scale_k, att_scale, att_bias)):
                    sp.dma_start(prow[0:1, j:j + 1], s).then_inc(consts_in, 16)
                sp.dma_start(xs[:], x_t).then_inc(x_in, 16)

                def section(n, t, s, odd, first=False, later=False, compact=None):
                    for i in range(16):
                        slot = (16 * odd + i) % RING
                        if not (first and i < RING):
                            sp.wait_ge(eq_ready, 16 * n + (i - RING + 1))
                            sp.wait_ge(sign_ready, 16 * n + (i - RING + 1))
                        sp.dma_start(ring[:, slot, :], adj_t[16 * t + i, :, bass.ds(s * SEC, SEC)])\
                            .then_inc(adj_in[slot], 16)
                over_sections(sp, section)

            NCONST = 16 * 18

            @block.scalar
            def _(act):
                act.wait_ge(params_bc, 1)
                act.activation(esc[:], par[:, 0:3], ACT.Exp).then_inc(exps_ready, 1)
                act.wait_ge(setup_done, 1)

                def turn_copy(c, turned_sem, copied_sem, dst):
                    act.wait_ge(S[turned_sem], c + 1)
                    act.activation(dst, work[0:D, :], ACT.Copy).then_inc(S[copied_sem], 1)

                def chunk_step(i, c):
                    if i == 1:
                        act.wait_ge(S["var_ready"], c + 1)
                        act.activation(st[:, 1, 0:CT], st[:, 0, 0:CT], ACT.Sqrt, bias=lneps[:, 0:1])\
                            .then_inc(S["std_ready"], 1)
                    if i == 3:
                        turn_copy(c, "nat_turned", "nat_copied", turned[0:D, :])
                    if i == 5:
                        act.wait_ge(S["hidden_copied"], c + 1)
                        act.activation(st[:, 2, 0:CT], hid[:, 0:CT, 0], ACT.Sigmoid)\
                            .then_inc(S["gate_ready"], 1)
                    if i == 6:
                        act.wait_ge(S["ratio_ready"], c + 1)
                        act.activation(st[:, 5, 0:CT], st[:, 4, 0:CT], ACT.Sqrt).then_inc(S["root_ready"], 1)
                    if i == 8:
                        turn_copy(c, "h_turned", "h_copied", turned[0:D, :])
                    if i == 10:
                        act.wait_ge(S["qk_copied"], c + 1)
                        act.activation(st[:, 2, :], hid[:, :, 0], ACT.Sigmoid)\
                            .then_inc(S["qk_gate_ready"], 1)
                    if i == 11:
                        act.wait_ge(S["qk_ratio_ready"], c + 1)
                        act.activation(st[:, 5, :], st[:, 4, :], ACT.Sqrt).then_inc(S["qk_root_ready"], 1)
                    if i == 13:
                        act.wait_ge(S["q_ready"], c + 1)
                        act.dma_start(table_t[:, bass.ds(c * CT, CT), :], kh[:]).then_inc(S["table_written"], 16)
                        turn_copy(c, "q_turned", "q_copied", qT[:, bass.ds(c * CT * P, CT * P)])

                def copy_signs(n):
                    act.wait_ge(packed, 16 * n + 16)
                    act.activation(differ[:], sign_ps[:], ACT.Copy).then_inc(S["signs_copied"], 1)

                def section(n, t, s, odd, first=False, later=False, compact=None):
                    for i in range(16):
                        slot, e = (16 * odd + i) % RING, i % EB
                        act.wait_ge(adj_in[slot], 16 * (2 * n + i // RING + 1))
                        if not (first and i < EB):
                            act.wait_ge(packed, 16 * n + (i - EB + 1))
                        act.activation(sgb[:, e, :], ring[:, slot, :], ACT.Sign).then_inc(sign_ready, 1)
                        if later:
                            act_batch(act, i, n - NS)
                        else:
                            chunk_step(i, n)
                        if i == 1 and not first:
                            copy_signs(n - 1)
                over_sections(act, section)
                copy_signs(SECT - 1)
                with act.Fori(NB - BPS, NB) as b:
                    for i in range(16):
                        act_batch(act, i, b)
                act.wait_ge(S["y_written"], 16 * NB)

            @block.tensor
            def _(pe):
                pe.wait_ge(consts_in, NCONST)
                for j in range(3):
                    pe.transpose(work[0:D, j * D:(j + 1) * D], wnat[:, j, :], ident[0:D, 0:D])
                pe.matmul(work[:, 512:512 + NPAR], ones[0:1, :], prow[:], start=True, stop=True)\
                    .then_inc(weights_T, 1)
                pe.wait_ge(setup_done, 1)

                def chunk_step(i, c, first):
                    if i == 2:
                        if not first:
                            pe.wait_ge(S["q_copied"], c)
                        turn(pe, lambda t: nat[:, t, :], c, "nat_ready", "nat_turned")
                    if i == 4:
                        pe.wait_ge(S["nat_copied"], c + 1)
                        for t in range(CT):
                            ins = pe.matmul(work[:, t * D:(t + 1) * D], turned[:, t * P:(t + 1) * P], w0a[:],
                                            start=True, stop=True)
                        ins.then_inc(S["hidden_ready"], 1)
                    if i == 8:
                        turn(pe, lambda t: kh[:, t, D:2 * D], c, "h_ready", "h_turned")
                    if i == 9:
                        pe.wait_ge(S["h_copied"], c + 1)
                        for t in range(CT):
                            ins = pe.matmul(work[:, t * 2 * D:(t + 1) * 2 * D], turned[:, t * P:(t + 1) * P],
                                            wqk[:], start=True, stop=True)
                        ins.then_inc(S["qk_ready"], 1)
                    if i == 13:
                        turn(pe, lambda t: nat[:, t, :], c, "q_ready", "q_turned")

                def turn_slots(t):
                    pe.wait_ge(S["slots_ready"], t + 1)
                    pe.wait_ge(S["q_copied"], NC)
                    pe.wait_ge(S["y_ready"], t * BPS)
                    for j, src in enumerate((colpad, bitpad)):
                        o = work[:, j * PAIRS:(j + 1) * PAIRS]
                        pe.matmul(o, src[:, SLOTS:3 * SLOTS], sel_even, start=True, stop=False)
                        ins = pe.matmul(o, src[:, 0:2 * SLOTS], sel_odd, start=False, stop=True)
                    ins.then_inc(S["slots_turned"], 1)

                def section(n, t, s, odd, first=False, later=False, compact=None):
                    for h in range(2):
                        cols = slice(h * 512, (h + 1) * 512)
                        if h == 0 and not first:
                            pe.wait_ge(section_read, n)
                        for o in (key_ps[odd], sign_ps):
                            pe.matmul(o[:, cols], ones_row, column_row[:, cols], start=True, stop=False)
                    for i in range(16):
                        e = i % EB
                        w = cb[:, 120 - 8 * i:248 - 8 * i]
                        pe.wait_ge(eq_ready, 16 * n + i + 1)
                        pe.wait_ge(sign_ready, 16 * n + i + 1)
                        for o, src in ((key_ps[odd], eqb), (sign_ps, sgb)):
                            for h in range(2):
                                cols = slice(h * 512, (h + 1) * 512)
                                ins = pe.matmul(o[:, cols], w, src[:, e, cols], start=False, stop=(i == 15))
                        ins.then_inc(packed, 1)
                        if i == 2 and compact is not None:
                            turn_slots(compact)
                        if later:
                            pe_batch(pe, i, n - NS, odd)
                        else:
                            chunk_step(i, n, first)
                over_sections(pe, section)
                turn_slots(ST - 1)
                with pe.Fori(0, BPS // 2) as k:
                    for odd in range(2):
                        for i in range(16):
                            pe_batch(pe, i, 2 * k + (NB - BPS) + odd, odd)
                pe.wait_ge(S["bad_ready"], 1)
                pe.wait_ge(S["y_ready"], NB)
                pe.matmul(work[0:1, 0:1], bad[:, 3:4], ones[:, 0:1], start=True, stop=True)\
                    .then_inc(S["flag_summed"], 1)

            @block.vector
            def _(dve):
                for t in (turned, colpad, bitpad, misrun, lneps):
                    ins = V.memset(t[:], 0.0)
                then(ins)
                V.memset(lneps[:], LN_EPS)
                V.memset(pturned[D:D + 1, :], 1.0)
                then(V.memset(turned[D:D + 1, :], 1.0))
                dve.wait_ge(weights_T, 1)
                V.tensor_copy(w0a[0:D, :], work[0:D, 0:D])
                V.tensor_copy(wqk[0:D, :], work[0:D, D:3 * D])
                V.tensor_copy(par[:], work[:, 512:512 + NPAR]).then_inc(params_bc, 1)
                dve.wait_ge(params_bc, 1)
                then(V.reciprocal(att_s[:, 2:3], par[:, 3:4]))
                then(V.tensor_scalar(att_s[:, 0:1], att_s[:, 2:3], 2.0, None, ALU.mult))
                V.tensor_tensor(att_s[:, 1:2], att_s[:, 0:1], par[:, 4:5], ALU.add)
                dve.wait_ge(exps_ready, 1)
                V.tensor_copy(esc_h[:], esc[:, 0:1].to_broadcast([P, CT]))
                V.tensor_copy(esc_qk[:, :, 0], esc[:, 1:2].to_broadcast([P, CT]))
                V.tensor_copy(esc_qk[:, :, 1], esc[:, 2:3].to_broadcast([P, CT]))
                V.memset(bad[:], 0.0).then_inc(setup_done, 1)

                def gate(g):
                    then(V.tensor_tensor(sqr[:, 0:g, 1:D], hid[:, 0:g, 1:D], hid[:, 0:g, 1:D], ALU.mult))
                    then(reduce_x(st[:, 6, 0:g], sqr[:, 0:g, 1:D]))
                    then(V.tensor_scalar(st[:, 6, 0:g], st[:, 6, 0:g], 1e-8, None, ALU.max))
                    then(V.reciprocal(st[:, 7, 0:g], st[:, 6, 0:g]))

                def gate_end(g, esct):
                    then(V.tensor_tensor(st[:, 3, 0:g], st[:, 2, 0:g], esct, ALU.mult))
                    then(V.tensor_scalar(st[:, 3, 0:g], st[:, 3, 0:g], 1.1, None, ALU.add))
                    then(V.tensor_tensor(st[:, 6, 0:g], st[:, 3, 0:g], st[:, 3, 0:g], ALU.mult))
                    then(V.tensor_scalar(st[:, 6, 0:g], st[:, 6, 0:g], -1.0, None, ALU.add))
                    return V.tensor_tensor(st[:, 4, 0:g], st[:, 6, 0:g], st[:, 7, 0:g], ALU.mult)

                def chunk_step(i, c, first):
                    rows = xs[:, bass.ds(c * CT, CT), :]
                    if i == 0:
                        if first:
                            dve.wait_ge(x_in, 16)
                        then(reduce_x(st[:, 6, 0:CT], rows))
                        then(V.tensor_scalar(st[:, 6, 0:CT], st[:, 6, 0:CT], 1.0 / D, None, ALU.mult))
                        then(V.tensor_tensor(hid[:, 0:CT, :], rows, bc(st[:, 6, 0:CT], CT), ALU.subtract))
                        then(V.tensor_tensor(sqr[:, 0:CT, :], hid[:, 0:CT, :], hid[:, 0:CT, :], ALU.mult))
                        then(reduce_x(st[:, 7, 0:CT], sqr[:, 0:CT, :]))
                        V.tensor_scalar(st[:, 0, 0:CT], st[:, 7, 0:CT], 1.0 / D, None, ALU.mult)\
                            .then_inc(S["var_ready"], 1)
                    if i == 2:
                        dve.wait_ge(S["std_ready"], c + 1)
                        then(V.reciprocal(st[:, 7, 0:CT], st[:, 1, 0:CT]))
                        if not first:
                            dve.wait_ge(S["q_turned"], c)
                        then(V.tensor_tensor(nat[:], hid[:, 0:CT, :], bc(st[:, 7, 0:CT], CT), ALU.mult))
                        V.tensor_scalar(nat[:], nat[:], 0.0, None, ALU.max).then_inc(S["nat_ready"], 1)
                    if i == 5:
                        dve.wait_ge(S["hidden_ready"], c + 1)
                        V.tensor_copy(hid[:, 0:CT, :], work[:, 0:CT * D].rearrange("p (t d) -> p t d", d=D))\
                            .then_inc(S["hidden_copied"], 1)
                        dve.wait_ge(S["hidden_copied"], c + 1)
                        gate(CT)
                    if i == 6:
                        dve.wait_ge(S["gate_ready"], c + 1)
                        gate_end(CT, esc_h[:]).then_inc(S["ratio_ready"], 1)
                    if i == 7:
                        dve.wait_ge(S["root_ready"], c + 1)
                        if not first:
                            dve.wait_ge(S["table_written"], 16 * c)
                        V.tensor_tensor(kh[:, :, D + 1:2 * D], hid[:, 0:CT, 1:D],
                                        st[:, 5, 0:CT].unsqueeze(2).to_broadcast([P, CT, D - 1]), ALU.mult)
                        V.tensor_copy(kh[:, :, D], st[:, 3, 0:CT]).then_inc(S["h_ready"], 1)
                    if i == 10:
                        dve.wait_ge(S["qk_ready"], c + 1)
                        V.tensor_copy(hid[:], work[:].rearrange("p (t d) -> p t d", d=D))\
                            .then_inc(S["qk_copied"], 1)
                        dve.wait_ge(S["qk_copied"], c + 1)
                        gate(2 * CT)
                    if i == 11:
                        dve.wait_ge(S["qk_gate_ready"], c + 1)
                        gate_end(2 * CT, esc_qk[:].rearrange("p a b -> p (a b)")).then_inc(S["qk_ratio_ready"], 1)
                    if i == 12:
                        dve.wait_ge(S["qk_root_ready"], c + 1)
                        root = st[:, 5, :].unsqueeze(2).to_broadcast([P, 2 * CT, D - 1])
                        V.tensor_tensor(nat[:, :, 1:D], hid[:, 0:2 * CT:2, 1:D], root[:, 0:2 * CT:2, :], ALU.mult)
                        V.tensor_tensor(kh[:, :, 1:D], hid[:, 1:2 * CT:2, 1:D], root[:, 1:2 * CT:2, :], ALU.mult)
                        V.tensor_copy(kh[:, :, 0], st[:, 3, 1:2 * CT:2])
                        V.tensor_scalar(nat[:, :, 0], st[:, 3, 0:2 * CT:2], -1.0, None, ALU.mult)\
                            .then_inc(S["q_ready"], 1)

                def read_section(n, s, odd):
                    dve.wait_ge(S["signs_copied"], n + 1)
                    V.tensor_tensor(differ[:], key_ps[odd][:], differ[:], ALU.not_equal)
                    for u in range(NSUB):
                        ins = V.max(best[:, odd, 8 * u:8 * u + 8], key_ps[odd][:, SUB * u:SUB * (u + 1)])
                    then(ins)
                    V.tensor_copy(cand[:, bass.ds(s * (NSUB * 8), NSUB * 8)], best[:, odd, :])
                    V.tensor_reduce(mis[:, odd:odd + 1], differ[:], AX.X, ALU.max).then_inc(section_read, 1)
                    dve.wait_ge(section_read, n + 1)
                    then(V.tensor_tensor(misrun[:], misrun[:], mis[:, odd:odd + 1], ALU.max))

                def compact_slots(t):
                    V.tensor_reduce(over[:, bass.ds(2 * t, 1)], cand[:, 7:NS * NSUB * 8:8], AX.X, ALU.max)
                    for r in range(SLOTS // 8):
                        e = slice(8 * r, 8 * r + 8)
                        then(V.max(key8[:, e], cand[:]))
                        then(V.max_index(pos8[:, e], key8[:, e], cand[:]))
                        then(V.match_replace(cand[:], key8[:, e], cand[:], -1.0))
                    V.tensor_copy(over[:, bass.ds(2 * t + 1, 1)], key8[:, SLOTS - 1:SLOTS])
                    then(V.tensor_copy(keyi[:], key8[:]))
                    V.tensor_scalar(lowi[:], keyi[:], SUB - 1, None, ALU.bitwise_and)
                    then(V.tensor_scalar(pos8[:], pos8[:], 3, SUBBITS, ALU.logical_shift_right,
                                         ALU.logical_shift_left))
                    then(V.tensor_scalar(keyi[:], keyi[:], SUBBITS, None, ALU.logical_shift_right))
                    V.tensor_tensor(colpad[:, SLOTS:2 * SLOTS], lowi[:], pos8[:].bitcast(I32), ALU.add)
                    V.tensor_copy(bitpad[:, SLOTS:2 * SLOTS], keyi[:]).then_inc(S["slots_ready"], 1)
                    dve.wait_ge(S["slots_turned"], t + 1)
                    V.tensor_copy(biti[:], work[:, PAIRS:2 * PAIRS])
                    then(V.tensor_copy(columns[:, bass.ds(t * PAIRS, PAIRS)], work[:, 0:PAIRS]))
                    half = PAIRS // 2
                    bits = differ[:].bitcast(I32)
                    for h in range(2):
                        then(V.tensor_tensor(
                            bits.rearrange("p (c r) -> p c r", r=32),
                            biti[:, h * half:(h + 1) * half].unsqueeze(2).to_broadcast([P, half, 32]),
                            ci[:].unsqueeze(1).to_broadcast([P, half, 32]), ALU.bitwise_and))
                        ins = V.tensor_scalar(mask[:, bass.ds(t * (PAIRS * 32) + h * half * 32, half * 32)], bits,
                                              1.0, None, ALU.min)
                        if h == 0:
                            then(ins)
                    ins.then_inc(S["columns_ready"], 1)

                def section(n, t, s, odd, first=False, later=False, compact=None):
                    for i in range(16):
                        slot, e = (16 * odd + i) % RING, i % EB
                        dve.wait_ge(adj_in[slot], 16 * (2 * n + i // RING + 1))
                        if not (first and i < EB):
                            dve.wait_ge(packed, 16 * n + (i - EB + 1))
                        V.tensor_scalar(eqb[:, e, :], ring[:, slot, :], 1.0, None, ALU.is_equal)\
                            .then_inc(eq_ready, 1)
                        if i == 2 and not first:
                            if compact is None:
                                read_section(n - 1, s - 1, 1 - odd)
                            else:
                                read_section(n - 1, NS - 1, 1)
                                compact_slots(compact)
                        if later:
                            dve_batch(dve, i, n - NS)
                        else:
                            chunk_step(i, n, first)
                over_sections(dve, section, [(step, *DVE_STEPS[0:2])])
                read_section(SECT - 1, NS - 1, 1)
                compact_slots(ST - 1)
                with dve.Fori(0, BPS) as b:
                    with step.loop(b, BPS, DVE_STEPS[2]):
                        for i in range(16):
                            dve_batch(dve, i, b + (NB - BPS))
                then(V.tensor_reduce(bad[:, 0:1], over[:], AX.X, ALU.max))
                then(V.tensor_scalar(bad[:, 1:2], bad[:, 0:1], float(SUB), None, ALU.is_ge))
                V.tensor_tensor(bad[:, 3:4], bad[:, 1:2], misrun[:], ALU.max).then_inc(S["bad_ready"], 1)
                dve.wait_ge(S["flag_summed"], 1)
                V.tensor_scalar(flag[:], work[0:1, 0:1], 1.0, None, ALU.min).then_inc(S["flag_ready"], 1)

            @block.gpsimd
            def _(pool):
                pool.wait_ge(S["table_written"], 16 * NC)

                for b in range(NB):
                    if b % BPS == 0:
                        pool.wait_ge(S["columns_ready"], b // BPS + 1)
                    if b >= 2:
                        pool.wait_ge(S["support_ready"], b - 1)
                    for q in range(PB):
                        column = columns[:, b * PB + q:b * PB + q + 1]
                        nc.gpsimd.indirect_dma_start(gat[:, b % 2, q, :], None, table[:, :],
                                                     bass.IndirectOffsetOnAxis(column, 0))\
                            .then_inc(gathered[b % 2], 16)

        def flagged(eng):
            return eng.value_load(flag[0:1, 0:1], min_val=0, max_val=1)

        class Dense:

            def __init__(self, tag, attention):
                self.attention = attention
                self.T = {k: sem(f"{tag}_{k}") for k in
                          ("rows_in", "x_in", "keys_turned", "keys_copied", "query_ready", "scores_ready",
                           "gate_ready", "weights_ready", "turned", "copied", "product_ready", "added")}
                self.block_in = [sem(f"{tag}_block_in_{i}") for i in range(2)]
                self.count = Count(sem(f"{tag}_dve_step"))

            def over_blocks(self, eng, before, body, count=None, per=0):
                with eng.Fori(0, N // SEC) as c:
                    with ExitStack() as outer:
                        if count:
                            outer.enter_context(count.loop(c, N // SEC, per * NT // 2))
                        before(c)
                        with eng.Fori(0, NT // 2) as k:
                            with ExitStack() as inner:
                                if count:
                                    inner.enter_context(count.loop(k, NT // 2, per))
                                for odd in range(2):
                                    body(c, 2 * k + odd, NT * c + 2 * k + odd, odd)

            def sync(self, sp):
                T = self.T
                if self.attention:
                    sp.dma_start(xs[:], x_t).then_inc(T["x_in"], 16)

                def load_rows(c):
                    sp.wait_ge(T["added"], NT * c + 2)
                    if self.attention:
                        src, dst = table_t[:, bass.ds(c * CT, CT), :], kh[:]
                    else:
                        src, dst = ytable_t[:, bass.ds(c * CT, CT), :], kh[:, :, D:2 * D]
                    sp.dma_start(dst, src).then_inc(T["rows_in"], 16)

                def load_block(c, t, m, odd):
                    sp.wait_ge(T["added"], m + 1)
                    sp.dma_start(ring[:, odd, :], adj_t[t, :, bass.ds(c * SEC, SEC)]).then_inc(self.block_in[odd], 16)
                self.over_blocks(sp, load_rows, load_block)

            def tensor(self, pe):
                T = self.T

                def turn_keys(c):
                    if self.attention:
                        pe.wait_ge(T["rows_in"], 16 * c + 16)
                        for u in range(CT):
                            if u == 0:
                                ins = pe.matmul(work[0:D, 0:P], kh[:, u, 0:D], ident, start=True, stop=True)
                            else:
                                ins = pe.transpose(work[0:D, u * P:(u + 1) * P], kh[:, u, 0:D], ident)
                        ins.then_inc(T["keys_turned"], 1)

                def multiply(c, t, m, odd):
                    src = ring[:, odd, :]
                    if self.attention:
                        src = differ[:]
                        pe.wait_ge(T["keys_copied"], c + 1)
                        pe.wait_ge(T["query_ready"], m + 1)
                        for h in range(2):
                            ins = pe.matmul(sign_ps[:, h * 512:(h + 1) * 512], att[0:D, 0:P],
                                            turned[0:D, h * 512:(h + 1) * 512], start=True, stop=True)
                        ins.then_inc(T["scores_ready"], 1)
                        pe.wait_ge(T["weights_ready"], m + 1)
                    else:
                        pe.wait_ge(self.block_in[odd], (m - odd) * 8 + 16)
                    for u in range(CT):
                        ins = pe.transpose(key_ps[0][:, u * P:(u + 1) * P], src[:, u * P:(u + 1) * P], ident)
                    ins.then_inc(T["turned"], 1)
                    pe.wait_ge(T["rows_in"], 16 * c + 16)
                    pe.wait_ge(T["copied"], m + 1)
                    for u in range(CT):
                        ins = pe.matmul(work[:, 0:D], wide[:, u * P:(u + 1) * P], kh[:, u, D:2 * D],
                                        start=(u == 0), stop=(u == CT - 1))
                    ins.then_inc(T["product_ready"], 1)
                    pe.wait_ge(T["added"], m + 3)
                self.over_blocks(pe, turn_keys, multiply)

            def scalar(self, act):
                T = self.T

                def copy_keys(c):
                    if self.attention:
                        act.wait_ge(T["keys_turned"], c + 1)
                        act.activation(turned[0:D, :], work[0:D, :], ACT.Copy).then_inc(T["keys_copied"], 1)

                def gate_block(c, t, m, odd):
                    if self.attention:
                        act.activation(att[0:D, 0:P], qT[:, bass.ds(t * P, P)], ACT.Copy)\
                            .then_inc(T["query_ready"], 1)
                        act.wait_ge(T["scores_ready"], m + 1)
                        act.activation(differ[:], sign_ps[:], ACT.Sigmoid, bias=att_s[:, 1:2],
                                       scale=att_s[:, 0:1]).then_inc(T["gate_ready"], 1)
                    act.wait_ge(T["turned"], m + 1)
                    act.activation(wide, key_ps[0][:], ACT.Copy).then_inc(T["copied"], 1)
                self.over_blocks(act, copy_keys, gate_block)

            def vector(self, dve):
                T, count = self.T, self.count
                if self.attention:
                    V.memset(deg[:], 0.0)
                V.memset(agg[:], 0.0).then_inc(T["added"], 1)
                V.memset(bad[:, 0:1], 0.0).then_inc(T["added"], 1)

                def add_block(c, t, m, odd):
                    if self.attention:
                        dve.wait_ge(self.block_in[odd], (m - odd) * 8 + 16)
                        then(reduce_x(bad[:, 1:2], ring[:, odd, :]), count)
                        V.tensor_tensor(deg[:, bass.ds(t, 1)], deg[:, bass.ds(t, 1)], bad[:, 1:2], ALU.add)
                        dve.wait_ge(T["gate_ready"], m + 1)
                        V.tensor_tensor(differ[:], differ[:], ring[:, odd, :], ALU.mult)\
                            .then_inc(T["weights_ready"], 1)
                    dve.wait_ge(T["product_ready"], m + 1)
                    V.tensor_tensor(agg[:, bass.ds(t, 1), :], agg[:, bass.ds(t, 1), :],
                                    work[:, 0:D].unsqueeze(1), ALU.add).then_inc(T["added"], 1)
                self.over_blocks(dve, lambda c: None, add_block, count, 2 * self.attention)
                dve.wait_ge(T["added"], NT * (N // SEC) + 2)

        wide = hid[:].rearrange("p t d -> p (t d)")
        first_layer = Dense("dense_0", True)
        with nc.Block() as block:
            @block.sync
            def _(sp):
                with sp.If(flagged(sp) > 0):
                    first_layer.sync(sp)
                    sp.nop()

            @block.tensor
            def _(pe):
                with pe.If(flagged(pe) > 0):
                    first_layer.tensor(pe)
                    with pe.Fori(0, NB) as b:
                        pe.wait_ge(S["y_ready"], b + NB)
                        for i in range(16):
                            pe_post(pe, i, b + NB)
                    pe.nop()

            @block.scalar
            def _(act):
                with act.If(flagged(act) > 0):
                    first_layer.scalar(act)
                    with act.Fori(0, NB) as b:
                        for i in range(16):
                            act_post(act, i, b, b + NB)
                    act.wait_ge(S["y_written"], 2 * 16 * NB)
                    act.nop()

            @block.vector
            def _(dve):
                with dve.If(flagged(dve) > 0):
                    first_layer.vector(dve)
                    dve.wait_ge(first_layer.T["x_in"], 16)
                    with dve.Fori(0, NB) as b:
                        with first_layer.count.loop(b, NB, POST_STEPS):
                            for i in range(16):
                                dve_post(dve, i, b, b + NB, first_layer.count)
                    dve.nop()

        second_layer = Dense("dense_1", False)
        names = ("mask_ready", "product_ready", "rows_done", "sum_ready", "total_ready", "centred",
                 "squares", "squares_sum", "var_ready_bn", "std_bn", "out_ready", "out_written")
        B = {k: sem(k) for k in names}
        ygathered = [sem(f"y_gathered_{i}") for i in range(2)]
        acc = psq
        flat = lambda a: a.rearrange("p t d -> p (t d)")

        with nc.Block() as block:
            @block.gpsimd
            def _(pool):
                with pool.If(flagged(pool) < 1):
                    for b in range(NB):
                        if b >= 2:
                            pool.wait_ge(B["product_ready"], b - 1)
                        for q in range(PB):
                            column = columns[:, b * PB + q:b * PB + q + 1]
                            nc.gpsimd.indirect_dma_start(ygat[:, b % 2, q, :], None, ytable[:, :],
                                                         bass.IndirectOffsetOnAxis(column, 0))\
                                .then_inc(ygathered[b % 2], 16)
                    pool.nop()

            @block.tensor
            def _(pe):
                with pe.If(flagged(pe) > 0):
                    second_layer.tensor(pe)
                    pe.nop()
                with pe.Else():
                    def product(b, odd, first=False):
                        pe.wait_ge(ygathered[odd], (b - odd) * (8 * PB) + 16 * PB)
                        pe.wait_ge(B["mask_ready"], b + 1)
                        if not first:
                            pe.wait_ge(B["rows_done"], b - 1)
                        for t in range(PB):
                            q, r = 32 * (t % 4), t // 4
                            ins = pe.matmul(work[q:q + 32, 512 * odd + r * D:512 * odd + (r + 1) * D],
                                            mstat[:, odd, t * 32:(t + 1) * 32], ygat[:, odd, t, :],
                                            start=True, stop=True, tile_position=(0, q))
                        ins.then_inc(B["product_ready"], 1)
                    product(0, 0, first=True)
                    product(1, 1, first=True)
                    with pe.Fori(1, NB // 2) as k:
                        for odd in range(2):
                            product(2 * k + odd, odd)
                    pe.nop()
                pe.wait_ge(B["sum_ready"], 1)
                pe.matmul(work[:, 0:TB * D], ones, flat(acc[:]), start=True, stop=True).then_inc(B["total_ready"], 1)
                for c in range(NC):
                    pe.wait_ge(B["squares"], c + 1)
                    ins = pe.matmul(work[:, 512:1024], ones, flat(ys[:, c * CT:(c + 1) * CT, :]),
                                    start=(c == 0), stop=(c == NC - 1))
                ins.then_inc(B["squares_sum"], 1)

            @block.scalar
            def _(act):
                with act.If(flagged(act) > 0):
                    second_layer.scalar(act)
                    act.nop()
                with act.Else():
                    def mask_of(b, odd, first=False):
                        if not first:
                            act.wait_ge(B["product_ready"], b - 1)
                        act.activation(mstat[:, odd, :], mask[:, bass.ds(b * (PB * 32), PB * 32)], ACT.Copy)\
                            .then_inc(B["mask_ready"], 1)
                    mask_of(0, 0, first=True)
                    mask_of(1, 1, first=True)
                    with act.Fori(1, NB // 2) as k:
                        for odd in range(2):
                            mask_of(2 * k + odd, odd)
                    act.nop()
                for c in range(NC):
                    r = slice(c * CT, (c + 1) * CT)
                    act.wait_ge(B["centred"], c + 1)
                    act.activation(ys[:, r, :], agg[:, r, :], ACT.Square).then_inc(B["squares"], 1)
                act.wait_ge(B["var_ready_bn"], 1)
                act.activation(bn[:, 2, :], bn[:, 1, :], ACT.Sqrt).then_inc(B["std_bn"], 1)
                act.wait_ge(B["std_bn"], 1)

            @block.vector
            def _(dve):
                then(V.memset(acc[:], 0.0))

                def rows_of(b, product, count):
                    rows = bass.ds(b * TB, TB)
                    then(V.tensor_tensor(pxc[:], product, ys[:, rows, :], ALU.add), count)
                    V.tensor_tensor(agg[:, rows, :], pxc[:], bc(dinv[:, rows], TB), ALU.mult)\
                        .then_inc(B["rows_done"], 1)
                    dve.wait_ge(B["rows_done"], b + 1)
                    then(V.tensor_tensor(acc[:], acc[:], agg[:, rows, :], ALU.add), count)
                with dve.If(flagged(dve) > 0):
                    second_layer.vector(dve)
                    with dve.Fori(0, NB) as b:
                        with second_layer.count.loop(b, NB, 2):
                            rows_of(b, agg[:, bass.ds(b * TB, TB), :], second_layer.count)
                    dve.nop()
                with dve.Else():
                    count = Count(sem("rows_step"))
                    with dve.Fori(0, NB // 2) as k:
                        with count.loop(k, NB // 2, 4):
                            for odd in range(2):
                                dve.wait_ge(B["product_ready"], 2 * k + odd + 1)
                                rows_of(2 * k + odd, work[:, 512 * odd:512 * odd + TB * D].rearrange(
                                    "p (t d) -> p t d", d=D), count)
                    dve.nop()
                V.memset(pst[:, 0, 0:1], 0.0).then_inc(B["sum_ready"], 1)
                dve.wait_ge(B["total_ready"], 1)
                then(V.tensor_copy(bn[:, 3:5, :], work[:, 0:TB * D].rearrange("p (t d) -> p t d", d=D)))
                then(V.tensor_tensor(bn[:, 0, :], bn[:, 3, :], bn[:, 4, :], ALU.add))
                then(V.tensor_scalar(bn[:, 0, :], bn[:, 0, :], 1.0 / N, None, ALU.mult))
                spread = lambda row: row.unsqueeze(1).to_broadcast([P, CT, D])
                for c in range(NC):
                    r = slice(c * CT, (c + 1) * CT)
                    V.tensor_tensor(agg[:, r, :], agg[:, r, :], spread(bn[:, 0, :]), ALU.subtract)\
                        .then_inc(B["centred"], 1)
                dve.wait_ge(B["squares_sum"], 1)
                then(V.tensor_reduce(bn[:, 5, :], work[:, 512:1024].rearrange("p (t d) -> p d t", d=D),
                                     AX.X, ALU.add))
                V.tensor_scalar(bn[:, 1, :], bn[:, 5, :], 1.0 / N, BN_EPS, ALU.mult, ALU.add)\
                    .then_inc(B["var_ready_bn"], 1)
                dve.wait_ge(B["std_bn"], 1)
                then(V.reciprocal(bn[:, 3, :], bn[:, 2, :]))
                then(V.tensor_tensor(bn[:, 4, :], bn[:, 3, :], par[:, 5:5 + D], ALU.mult))
                for c in range(NC):
                    r = slice(c * CT, (c + 1) * CT)
                    a = agg[:, r, :]
                    then(V.tensor_tensor(a, a, spread(bn[:, 4, :]), ALU.mult))
                    then(V.tensor_tensor(a, a, spread(par[:, 5 + D:5 + 2 * D]), ALU.add))
                    then(V.scalar_tensor_tensor(out=a, in0=a, scalar=SLOPE, in1=a, op0=ALU.mult, op1=ALU.max))
                    V.tensor_tensor(xs[:, r, :], xs[:, r, :], a, ALU.add).then_inc(B["out_ready"], 1)

            @block.sync
            def _(sp):
                with sp.If(flagged(sp) > 0):
                    second_layer.sync(sp)
                    sp.nop()
                for c in range(NC):
                    sp.wait_ge(B["out_ready"], c + 1)
                    sp.dma_start(out_t[:, c * CT:(c + 1) * CT, :], xs[:, c * CT:(c + 1) * CT, :])\
                        .then_inc(B["out_written"], 16)
                sp.wait_ge(B["out_written"], 16 * NC)


POST_STEPS = 14
DVE_STEPS = (50, 36, 16)

_INS = ["x", "adj", "L0_gnn_W", "L0_gnn_b", "L0_gnn_scale", "L0_gnn_Wq", "L0_gnn_bq", "L0_gnn_scale_q",
        "L0_gnn_Wk", "L0_gnn_bk", "L0_gnn_scale_k", "L0_gnn_att_bias", "L0_gnn_att_scale",
        "L1_gnn_W", "L1_gnn_b", "L1_gnn_gamma", "L1_gnn_beta"]


def kernel(**inputs):
    import numpy as np
    import concourse.bacc as bacc
    from concourse.bass_utils import run_bass_kernel_spmd

    nc = bacc.Bacc("TRN2", target_bir_lowering=False, num_devices=1)
    arrays, args = {}, []
    laid = {name: np.ascontiguousarray(inputs[name]) for name in _INS}
    for name, a in laid.items():
        if a.ndim == 0:
            laid[name] = a.reshape(1, 1)
    for name, a in {**laid, **host_constants(laid["x"].shape[0])}.items():
        arrays[f"in_{name}"] = a
        args.append(nc.dram_tensor(f"in_{name}", a.shape, mybir.dt.from_np(a.dtype), kind="ExternalInput").ap())
    out = nc.dram_tensor("out_0", laid["x"].shape, F32, kind="ExternalOutput").ap()
    graph_layers(nc, *args, out)
    r = run_bass_kernel_spmd(nc, [arrays], core_ids=[0])
    return r.results[0]["out_0"]
```

```python
from contextlib import ExitStack, contextmanager

import concourse.bass as bass
from concourse import mybir

P = 128
ALU = mybir.AluOpType
ACT = mybir.ActivationFunctionType
AX = mybir.AxisListType
F32 = mybir.dt.float32
BF16 = mybir.dt.bfloat16
I32 = mybir.dt.int32
U32 = mybir.dt.uint32
U8 = mybir.dt.uint8

GR = 16
SEC = 1024
SUB = 128
SUBBITS = 7
NSUB = SEC // SUB
SLOTS = 64
RING = 16
EB = 4
PB = 8
TB = 2
CT = 8
LN_EPS = 1e-5
BN_EPS = 1e-5
SLOPE = 0.01


class Count:

    def __init__(self, sem):
        self.sem, self.done, self.off = sem, 0, 0

    def inc(self, ins, by=1):
        ins.then_inc(self.sem, by)
        self.done += by

    def now(self):
        return self.off + self.done

    @contextmanager
    def loop(self, i, trips, per):
        outer, start = self.off, self.done
        self.off = outer + i * per
        yield
        assert self.done - start == per, (self.done - start, per)
        self.off, self.done = outer, start + trips * per


def host_constants(n):
    import numpy as np

    f = np.zeros((P, P + P + 2 * SLOTS), np.float32)
    f[:, 0:P] = np.eye(P)
    f[:, P:2 * P] = 1.0
    for c in range(SLOTS):
        f[2 * c, 2 * P + c] = 1.0
        f[2 * c + 1, 2 * P + SLOTS + c] = 1.0
    b = np.zeros((P, 248 + P + SEC), np.float32)
    for p in range(P):
        b[p, 120 + p // GR] = 2.0 ** (p % GR + SUBBITS)
    b[0, 248:248 + P] = 1.0
    b[0, 248 + P:] = np.arange(SEC) % SUB
    i = np.zeros((P, 2 * GR), np.int32)
    for p in range(P):
        h = p // SLOTS
        i[p, h * GR:(h + 1) * GR] = 2 ** np.arange(GR)
    halves = np.ascontiguousarray(b.view(np.uint16)[:, 1::2])
    return {"const_f": f, "const_b": halves, "const_i": i}


def graph_layers(nc, x, adj, W0, b0, scale0, Wq, bq, scale_q, Wk, bk, scale_k, att_bias, att_scale,
                 W1, b1, gamma, beta, const_f, const_b, const_i, out):
    N, D = x.shape
    NT = N // P
    ST = NT // 16
    NS = N // SEC
    SECT = ST * NS
    BPS = 16 // TB
    NB = ST * BPS
    PAIRS = 64
    NC = NT // CT
    assert NS == BPS == NC == 8 and D == 64

    table = nc.dram_tensor("key_and_h_table", [N, 2 * D], F32).ap()
    ytable = nc.dram_tensor("y_table", [N, D], F32).ap()
    table_t = table.rearrange("(t p) d -> p t d", p=P)
    ytable_t = ytable.rearrange("(t p) d -> p t d", p=P)
    adj_t = adj.rearrange("(t p) n -> t p n", p=P)
    x_t = x.rearrange("(t p) d -> p t d", p=P)
    out_t = out.rearrange("(t p) d -> p t d", p=P)

    with ExitStack() as ctx:
        def sb(name, shape, dt=F32):
            return ctx.enter_context(nc.sbuf_tensor(name, shape, dt))

        def sem(name):
            return ctx.enter_context(nc.semaphore(name))

        xs = sb("x_rows", [P, NT, D])
        ys = sb("y_rows", [P, NT, D])
        deg = sb("degree", [P, NT])
        dinv = sb("inv_sqrt_degree", [P, NT])
        qT = sb("q_transposed", [D, N])
        mask = sb("slot_mask", [P, ST * PAIRS * 32], U8)
        columns = sb("slot_columns", [P, ST * PAIRS], I32)
        ring = sb("adj_ring", [P, RING, SEC])
        agg = ring[:, RING // 2:RING // 2 + NT * D // SEC, :].rearrange("p a (t d) -> p (a t) d", d=D)
        eqb = sb("adj_is_one", [P, EB, SEC], BF16)
        absb = sb("adj_abs", [P, 2, SEC], BF16)
        rowsum = sb("row_sums", [P, SECT * 16])
        wide_a = sb("wide_scratch", [P, SEC])
        best = sb("best_of_subsections", [P, 2, NSUB * 8])
        cand = sb("candidates", [P, NS * NSUB * 8])
        key8 = sb("slot_keys", [P, SLOTS])
        pos8 = sb("slot_positions", [P, SLOTS], U32)
        keyi = sb("slot_keys_int", [P, SLOTS], I32)
        lowi = sb("column_in_subsection", [P, SLOTS], I32)
        colpad = sb("columns_padded", [P, 3 * SLOTS])
        bitpad = sb("bits_padded", [P, 3 * SLOTS])
        biti = sb("slot_bits", [P, PAIRS], I32)
        over = sb("overflow", [P, 2 * ST])
        total = sb("row_totals", [P, NT])
        bad = sb("bad", [P, 4])
        flag = sb("flag", [1, 1], I32)
        gat = sb("gathered", [P, 2, PB, 2 * D])
        ygat = gat[:, :, :, 0:D]
        att = sb("attention", [P, PB * 32])
        mstat = sb("batch_mask", [P, 2, PB * 32])
        attm = sb("attention_masked", [P, PB * 32])
        nat = sb("chunk_rows", [P, CT, D])
        centred = sb("chunk_centred", [P, CT, D])
        q_rows = sb("chunk_q_rows", [P, CT, D])
        kh_of = [gat[:, j, :, :] for j in range(2)]
        kh = kh_of[0]
        support = sb("batch_support", [P, 2, TB, D])
        sqr = wide_a[:].rearrange("p (t d) -> p t d", d=D)
        turned = sb("chunk_transposed", [D + 1, CT * P])
        keyT = turned[0:D, :]
        pnat = sb("batch_rows", [P, TB, D])
        psq = sb("batch_squares", [P, TB, D])
        pxc = sb("batch_centred", [P, TB, D])
        pturned = sb("batch_transposed", [D + 1, TB * P])
        pst = sb("batch_stats", [P, 6, 2 * TB])
        h_turned = sb("chunk_h_transposed", [D + 1, CT * P])
        st = sb("chunk_stats", [P, 8, CT])
        stqk = sb("chunk_stats_qk", [P, 8, 2 * CT])
        w0a = sb("w0_aug", [D + 1, D])
        wqk = sb("wqk_aug", [D + 1, 2 * D])
        w1a = sb("w1_aug", [D + 1, D])
        wnat = sb("w_natural", [D, 3, D])
        cf = sb("const_f_sb", [P, 2 * P + 2 * SLOTS])
        cb = sb("const_b_sb", [P, 248 + P + SEC], BF16)
        ci = sb("const_i_sb", [P, 2 * GR], I32)
        NPAR = 5 + 2 * D
        prow = sb("param_row", [1, NPAR])
        par = sb("params", [P, NPAR])
        esc = sb("exp_scales", [P, 3])
        esc_h = sb("exp_scale_h", [P, CT])
        esc_qk = sb("exp_scale_qk", [P, CT, 2])
        att_s = sb("att_scale_bias", [P, 4])
        bn = sb("bn_vectors", [P, 6, D])
        lneps = sb("ln_eps", [P, 1])

        key_ps = [ctx.enter_context(nc.psum_tensor(f"packed_ones_{i}", [P, SEC], F32)) for i in range(2)]
        side_ps = ctx.enter_context(nc.psum_tensor("side_work", [P, 1024], F32))
        slot_ps, post_ps = side_ps[:, 0:512], side_ps[:, 512:1024]
        work = ctx.enter_context(nc.psum_tensor("work", [P, 1024], F32))

        ident = cf[:, 0:P]
        ones = cf[:, P:2 * P]
        sel_even = cf[:, 2 * P:2 * P + SLOTS]
        sel_odd = cf[:, 2 * P + SLOTS:2 * P + 2 * SLOTS]
        ones_row = cb[:, 248:248 + P]
        column_row = cb[:, 248 + P:248 + P + SEC]

        consts_in = sem("consts_in")
        x_in = sem("x_in")
        adj_in = [sem(f"adj_in_{i}") for i in range(RING)]
        eq_ready = sem("eq_ready")
        row_summed = sem("row_summed")
        packed = sem("packed")
        section_read = sem("section_read")
        weights_T = sem("weights_T")
        params_bc = sem("params_broadcast")
        exps_ready = sem("exps_ready")
        setup_done = sem("setup_done")
        dve_step = sem("dve_step")
        names = ("var_ready", "std_ready", "nat_ready", "nat_turned", "nat_copied", "hidden_ready",
                 "gate_ready", "ratio_ready", "root_ready", "h_ready", "h_turned", "h_copied", "qk_ready",
                 "qk_gate_ready", "qk_ratio_ready", "qk_root_ready", "q_ready", "q_turned", "q_copied",
                 "table_written", "slots_ready", "slots_turned", "columns_ready",
                 "keys_turned", "keys_copied", "scores_ready", "att_ready", "attm_ready",
                 "support_ready", "support_copied", "norm_ready", "norm_root", "x1_var", "x1_std", "x1_nat",
                 "x1_turned", "x1_copied", "xw_ready", "y_ready", "y_written", "bad_ready", "flag_summed",
                 "flag_ready")
        S = {k: sem(k) for k in names}
        gathered = [sem(f"gathered_{i}") for i in range(2)]

        def over_sections(eng, section, counters=()):
            @contextmanager
            def counted(i, trips, column):
                with ExitStack() as s:
                    for c, *per in counters:
                        s.enter_context(c.loop(i, trips, per[column]))
                    yield
            section(0, 0, 0, 0, first=True)
            section(1, 0, 1, 1)
            with eng.Fori(0, NS // 2 - 1) as k:
                with counted(k, NS // 2 - 1, 0):
                    for odd in range(2):
                        section(2 * k + 2 + odd, 0, 2 * k + 2 + odd, odd)
            for t in range(1, ST):
                for odd in range(2):
                    section(NS * t + odd, t, odd, odd, later=True, compact=(t - 1 if odd == 0 else None))
                with eng.Fori(0, NS // 2 - 1) as k:
                    with counted(k, NS // 2 - 1, 1):
                        for odd in range(2):
                            section(2 * k + NS * t + 2 + odd, t, 2 * k + 2 + odd, odd, later=True)

        def first_later(n):
            return isinstance(n, int) and n == NS

        def batches_beside(n, odd, first, second, finish):
            if first_later(n):
                finish(n - 1, 1 - odd)
                return
            if not (isinstance(n, int) and n == NS + 1):
                second(n - NS - 2, odd)
            first(n - NS - 1, 1 - odd)

        def reduce_x(dst, src, op=ALU.add):
            return nc.vector.tensor_reduce(dst, src, AX.X, op)

        def bc(col, g):
            return col.unsqueeze(2).to_broadcast([P, g, D])

        V = nc.vector
        step = Count(dve_step)

        def then(ins, count=step):
            count.inc(ins)
            nc.vector.wait_ge(count.sem, count.now())

        def turn(pe, src, c, ready, done, count=CT, dst=work):
            if ready:
                pe.wait_ge(S[ready], c + 1)
            for t in range(count):
                if t == 0:
                    pe.matmul(dst[0:D, 0:P], src(t), ident, start=True, stop=True)
                    continue
                ins = pe.transpose(dst[0:D, t * P:(t + 1) * P], src(t), ident)
            ins.then_inc(S[done], 1)

        def pe_first(pe, i, b, odd, place=work):
            if i == 13:
                pe.wait_ge(gathered[odd], (b - odd) * (8 * PB) + 16 * PB)
                if isinstance(b, int) and b == 0:
                    pe.wait_ge(S["q_copied"], NC)
                elif place is work:
                    pe.wait_ge(S["support_copied"], b)
                turn(pe, lambda t: gat[:, odd, t, 0:D], b, None, "keys_turned", PB, place)
            if i == 15:
                pe.wait_ge(S["keys_copied"], b + 1)
                for t in range(PB):
                    ins = pe.matmul(place[:, t * 32:(t + 1) * 32], keyT[:, t * P:(t + 1) * P],
                                    qT[:, bass.ds(b * (PB * 32) + t * 32, 32)], start=True, stop=True)
                ins.then_inc(S["scores_ready"], 1)

        def pe_second(pe, i, b, odd):
            if i == 2:
                pe.wait_ge(S["attm_ready"], b + 1)
                for t in range(PB):
                    q, r = 32 * (t % 4), t // 4
                    pe.matmul(work[q:q + 32, 512 + r * D:512 + (r + 1) * D], attm[:, t * 32:(t + 1) * 32],
                              gat[:, odd, t, D:2 * D], start=True, stop=True, tile_position=(0, q))
                    ins = pe.matmul(work[q:q + 32, 512 + TB * D + r:512 + TB * D + r + 1],
                                    mstat[:, 0, t * 32:(t + 1) * 32], ones[:, 0:1],
                                    start=True, stop=True, tile_position=(0, q))
                ins.then_inc(S["support_ready"], 1)

        def act_first(act, i, b, place=work):
            if i == 14:
                act.wait_ge(S["keys_turned"], b + 1)
                act.activation(keyT[:], place[0:D, :], ACT.Copy).then_inc(S["keys_copied"], 1)

        def act_second(act, i, b, place=work):
            if i == 0:
                act.wait_ge(S["scores_ready"], b + 1)
                act.activation(att[:], place[:, 0:PB * 32], ACT.Sigmoid, bias=att_s[:, 1:2],
                               scale=att_s[:, 0:1]).then_inc(S["att_ready"], 1)

        def dve_second(dve, i, b, dst):
            if i == 0:
                then(V.tensor_copy(mstat[:, 0, :], mask[:, bass.ds(b * (PB * 32), PB * 32)]))
            if i == 1:
                dve.wait_ge(S["att_ready"], b + 1)
                V.tensor_tensor(attm[:], att[:], mstat[:, 0, :], ALU.mult).then_inc(S["attm_ready"], 1)
            if i == 4:
                dve.wait_ge(S["support_ready"], b + 1)
                V.tensor_copy(deg[:, bass.ds(b * TB, TB)], work[:, 512 + TB * D:512 + TB * D + TB])
                V.tensor_copy(dst, work[:, 512:512 + TB * D].rearrange("p (t d) -> p t d", d=D))\
                    .then_inc(S["support_copied"], 1)
                dve.wait_ge(S["support_copied"], b + 1)

        class Nodes:

            def __init__(self, g, squares, centred, rows, turned, stats, turn_psum, product_psum):
                self.g, self.sq, self.xc, self.rows, self.turned, self.st = g, squares, centred, rows, turned, stats
                self.turn_psum, self.product_psum = turn_psum, product_psum

            def tensor(self, pe, i, m):
                if i == 9:
                    pe.wait_ge(S["x1_nat"], m + 1)
                    for t in range(self.g):
                        dst = self.turn_psum[t // 4][0:D, (t % 4) * P:(t % 4 + 1) * P]
                        if t == 0:
                            pe.matmul(dst, self.rows[:, t, :], ident, start=True, stop=True)
                            continue
                        ins = pe.transpose(dst, self.rows[:, t, :], ident)
                    ins.then_inc(S["x1_turned"], 1)
                if i == 12:
                    pe.wait_ge(S["x1_copied"], m + 1)
                    for t in range(self.g):
                        ins = pe.matmul(self.product_psum[:, t * D:(t + 1) * D],
                                        self.turned[:, t * P:(t + 1) * P], w1a[:], start=True, stop=True)
                    ins.then_inc(S["xw_ready"], 1)

            def scalar(self, act, i, t0, m):
                g, st = self.g, self.st
                if i == 5:
                    act.wait_ge(S["norm_ready"], m + 1)
                    act.activation(st[:, 1, :], st[:, 0, :], ACT.Sqrt).then_inc(S["norm_root"], 1)
                if i == 7:
                    act.wait_ge(S["x1_var"], m + 1)
                    act.activation(st[:, 3, 0:g], st[:, 2, 0:g], ACT.Sqrt, bias=lneps[:, 0:1])\
                        .then_inc(S["x1_std"], 1)
                if i == 11:
                    act.wait_ge(S["x1_turned"], m + 1)
                    for h in range(0, g, 4):
                        w = min(g, 4) * P
                        ins = act.activation(self.turned[0:D, h * P:h * P + w], self.turn_psum[h // 4][0:D, 0:w],
                                             ACT.Relu)
                    ins.then_inc(S["x1_copied"], 1)
                if i == 15:
                    act.wait_ge(S["y_ready"], m + 1)
                    act.dma_start(ytable_t[:, bass.ds(t0, g), :], ys[:, bass.ds(t0, g), :])\
                        .then_inc(S["y_written"], 16)

            def vector(self, dve, i, t0, m, src, count=step):
                g, st, sq, xc = self.g, self.st, self.sq, self.xc
                rows = bass.ds(t0, g)
                link = lambda ins: then(ins, count)
                if i == 4:
                    link(V.tensor_tensor(sq, src, src, ALU.mult))
                    V.tensor_scalar(st[:, 0, g:2 * g], deg[:, rows], 1.0, None, ALU.add)
                    link(reduce_x(st[:, 4, 0:g], sq[:, :, 1:D]))
                    link(V.tensor_tensor(st[:, 4, g:2 * g], st[:, 4, 0:g], sq[:, :, 0], ALU.subtract))
                    link(V.scalar_tensor_tensor(out=st[:, 4, 0:g], in0=st[:, 4, g:2 * g], scalar=-1.0,
                                                in1=st[:, 4, g:2 * g], op0=ALU.mult, op1=ALU.max))
                    V.tensor_scalar(st[:, 0, 0:g], st[:, 4, 0:g], 1e-8, None, ALU.max)\
                        .then_inc(S["norm_ready"], 1)
                if i == 6:
                    dve.wait_ge(S["norm_root"], m + 1)
                    link(V.reciprocal(st[:, 4, :], st[:, 1, :]))
                    V.tensor_copy(dinv[:, rows], st[:, 4, g:2 * g])
                    link(V.tensor_tensor(xc, src, bc(st[:, 4, 0:g], g), ALU.mult))
                    link(V.tensor_tensor(sq, xs[:, rows, :], xc, ALU.add))
                    reduce_x(st[:, 5, 0:g], sq)
                    link(V.tensor_copy(xs[:, rows, :], sq))
                    link(V.tensor_scalar(st[:, 5, 0:g], st[:, 5, 0:g], 1.0 / D, None, ALU.mult))
                    link(V.tensor_tensor(xc, sq, bc(st[:, 5, 0:g], g), ALU.subtract))
                    link(V.tensor_tensor(sq, xc, xc, ALU.mult))
                    link(reduce_x(st[:, 5, g:2 * g], sq))
                    V.tensor_scalar(st[:, 2, 0:g], st[:, 5, g:2 * g], 1.0 / D, None, ALU.mult)\
                        .then_inc(S["x1_var"], 1)
                if i == 8:
                    dve.wait_ge(S["x1_std"], m + 1)
                    link(V.reciprocal(st[:, 5, 0:g], st[:, 3, 0:g]))
                    V.tensor_tensor(self.rows, xc, bc(st[:, 5, 0:g], g), ALU.mult).then_inc(S["x1_nat"], 1)
                if i == 13:
                    dve.wait_ge(S["xw_ready"], m + 1)
                    V.tensor_tensor(ys[:, rows, :], self.product_psum.rearrange("p (t d) -> p t d", d=D),
                                    bc(dinv[:, rows], g), ALU.mult).then_inc(S["y_ready"], 1)

        nodes = Nodes(TB, psq[:], pxc[:], pnat[:], pturned, pst, [post_ps], post_ps[:, 0:TB * D])

        TURN_SLOTS = EB + SLOTS // 8 + 1
        LAST = NB - BPS
        GROUP = 8
        at = lambda slot, shape: ring[:, slot, 0:shape[0] * shape[1]].rearrange("p (a b) -> p a b", b=shape[1])
        last_support = at(0, (16, D))
        last_nodes = Nodes(GROUP, at(1, (GROUP, D)), at(2, (GROUP, D)), at(3, (GROUP, D)), ring[0:D + 1, 4, :],
                           at(5, (6, 2 * GROUP)), [post_ps, slot_ps], work[:, 0:GROUP * D])
        POSTS = LAST + 16 // GROUP

        def last_batches(first, second, node):
            for a in range(LAST, NB):
                for i in range(16):
                    second(i, a, key_ps[a % 2])
                for i in range(16):
                    if a + 1 < NB:
                        first(i, a + 1, key_ps[(a + 1) % 2])
                half = a - LAST - 4
                if half in (0, 1):
                    for i in range(8 * half, 8 * half + 8):
                        node(i, LAST * TB, LAST, 0)
            for i in range(16):
                node(i, LAST * TB + GROUP, LAST + 1, GROUP)

        with nc.Block() as block:
            @block.sync
            def _(sp):
                for dst, src in ((cf[:], const_f), (cb[:], const_b.bitcast(BF16)), (ci[:], const_i),
                                 (wnat[:, 0, :], W0), (wnat[:, 1, :], Wq), (wnat[:, 2, :], Wk),
                                 (w1a[0:D, :], W1),
                                 (w0a[D:D + 1, :], b0.rearrange("(a d) -> a d", a=1)),
                                 (wqk[D:D + 1, 0:D], bq.rearrange("(a d) -> a d", a=1)),
                                 (wqk[D:D + 1, D:2 * D], bk.rearrange("(a d) -> a d", a=1)),
                                 (w1a[D:D + 1, :], b1.rearrange("(a d) -> a d", a=1)),
                                 (prow[0:1, 5:5 + D], gamma.rearrange("(a d) -> a d", a=1)),
                                 (prow[0:1, 5 + D:5 + 2 * D], beta.rearrange("(a d) -> a d", a=1))):
                    sp.dma_start(dst, src).then_inc(consts_in, 16)
                for j, s in enumerate((scale0, scale_q, scale_k, att_scale, att_bias)):
                    sp.dma_start(prow[0:1, j:j + 1], s).then_inc(consts_in, 16)
                sp.dma_start(xs[:], x_t).then_inc(x_in, 16)

                def section(n, t, s, odd, first=False, later=False, compact=None):
                    for i in range(16):
                        slot = (16 * odd + i) % RING
                        if not (first and i < RING):
                            sp.wait_ge(eq_ready, 16 * n + (i - RING + 1))
                            sp.wait_ge(row_summed, 16 * n + (i - RING + 1))
                        sp.dma_start(ring[:, slot, :], adj_t[16 * t + i, :, bass.ds(s * SEC, SEC)])\
                            .then_inc(adj_in[slot], 16)
                over_sections(sp, section)

            NCONST = 16 * 18

            @block.scalar
            def _(act):
                act.wait_ge(params_bc, 1)
                act.activation(esc[:], par[:, 0:3], ACT.Exp).then_inc(exps_ready, 1)
                act.wait_ge(setup_done, 1)

                def turn_copy(c, turned_sem, copied_sem, dst):
                    act.wait_ge(S[turned_sem], c + 1)
                    act.activation(dst, work[0:D, :], ACT.Copy).then_inc(S[copied_sem], 1)

                def hidden_step(i, c):
                    if i == 2:
                        act.wait_ge(S["var_ready"], c + 1)
                        act.activation(st[:, 1, :], st[:, 0, :], ACT.Sqrt, bias=lneps[:, 0:1])\
                            .then_inc(S["std_ready"], 1)
                    if i == 5:
                        act.wait_ge(S["nat_turned"], c + 1)
                        act.activation(turned[0:D, :], side_ps[0:D, :], ACT.Relu).then_inc(S["nat_copied"], 1)
                    if i == 8:
                        act.wait_ge(S["hidden_ready"], c + 1)
                        w = slot_ps.rearrange("p (t d) -> p t d", d=D)
                        act.activation(centred[:], w, ACT.Square)
                        act.activation(st[:, 2, :], w[:, :, 0], ACT.Sigmoid).then_inc(S["gate_ready"], 1)
                    if i == 11:
                        act.wait_ge(S["ratio_ready"], c + 1)
                        act.activation(st[:, 5, :], st[:, 4, :], ACT.Sqrt).then_inc(S["root_ready"], 1)

                def table_step(i, c, par):
                    if i == 3:
                        turn_copy(c, "h_turned", "h_copied", h_turned[0:D, :])
                    if i == 8:
                        act.wait_ge(S["qk_ready"], c + 1)
                        w = work[:].rearrange("p (t d) -> p t d", d=D)
                        act.activation(sqr, w, ACT.Square)
                        act.activation(stqk[:, 2, :], w[:, :, 0], ACT.Sigmoid).then_inc(S["qk_gate_ready"], 1)
                    if i == 12:
                        act.wait_ge(S["qk_ratio_ready"], c + 1)
                        act.activation(stqk[:, 5, :], stqk[:, 4, :], ACT.Sqrt).then_inc(S["qk_root_ready"], 1)
                    if i == 14:
                        act.wait_ge(S["q_ready"], c + 1)
                        act.dma_start(table_t[:, bass.ds(c * CT, CT), :], kh_of[par])\
                            .then_inc(S["table_written"], 16)
                    if i == 15:
                        turn_copy(c, "q_turned", "q_copied", qT[:, bass.ds(c * CT * P, CT * P)])

                def act_batch(i, b, t0):
                    act_second(act, i, b)
                    nodes.scalar(act, i, t0, b)

                def section(n, t, s, odd, first=False, later=False, compact=None):
                    for i in range(16):
                        slot, e = (16 * odd + i) % RING, i % EB
                        act.wait_ge(adj_in[slot], 16 * n + 16)
                        if not (first and i < 2):
                            act.wait_ge(row_summed, 16 * n + i - 1)
                        act.activation(absb[:, i % 2, :], ring[:, slot, :], ACT.Abs,
                                       accum_out=rowsum[:, bass.ds(16 * n + i, 1)]).then_inc(row_summed, 1)
                        if later:
                            batches_beside(n, odd, lambda b, par: act_first(act, i, b),
                                           lambda b, par: act_batch(i, b, n * TB - (NS + 2) * TB),
                                           lambda c, par: table_step(i, c, par))
                        else:
                            hidden_step(i, n)
                            if not first:
                                table_step(i, n - 1, 1 - odd)
                over_sections(act, section)
                for i in range(16):
                    act_batch(i, LAST - 2, (LAST - 2) * TB)
                    act_first(act, i, LAST - 1)
                for i in range(16):
                    act_batch(i, LAST - 1, (LAST - 1) * TB)
                    act_first(act, i, LAST, key_ps[LAST % 2])
                last_batches(lambda i, b, place: act_first(act, i, b, place),
                             lambda i, b, place: act_second(act, i, b, place),
                             lambda i, t0, m, at: last_nodes.scalar(act, i, t0, m))
                act.wait_ge(S["y_written"], 16 * POSTS)

            @block.tensor
            def _(pe):
                pe.wait_ge(consts_in, NCONST)
                for j in range(3):
                    pe.transpose(work[0:D, j * D:(j + 1) * D], wnat[:, j, :], ident[0:D, 0:D])
                pe.matmul(work[:, 512:512 + NPAR], ones[0:1, :], prow[:], start=True, stop=True)\
                    .then_inc(weights_T, 1)
                pe.wait_ge(setup_done, 1)

                def hidden_step(i, c, par):
                    if i == 4:
                        turn(pe, lambda t: nat[:, t, :], c, "nat_ready", "nat_turned", dst=side_ps)
                    if i == 6:
                        pe.wait_ge(S["nat_copied"], c + 1)
                        for t in range(CT):
                            ins = pe.matmul(slot_ps[:, t * D:(t + 1) * D], turned[:, t * P:(t + 1) * P], w0a[:],
                                            start=True, stop=True)
                        ins.then_inc(S["hidden_ready"], 1)

                def table_step(i, c, par):
                    if i == 1:
                        if not (isinstance(c, int) and c == 0):
                            pe.wait_ge(S["q_copied"], c)
                        turn(pe, lambda t: kh_of[par][:, t, D:2 * D], c, "h_ready", "h_turned")
                    if i == 5:
                        pe.wait_ge(S["h_copied"], c + 1)
                        for t in range(CT):
                            ins = pe.matmul(work[:, t * 2 * D:(t + 1) * 2 * D], h_turned[:, t * P:(t + 1) * P],
                                            wqk[:], start=True, stop=True)
                        ins.then_inc(S["qk_ready"], 1)
                    if i == 14:
                        turn(pe, lambda t: q_rows[:, t, :], c, "q_ready", "q_turned")

                def turn_slots(t):
                    pe.wait_ge(S["slots_ready"], t + 1)
                    for j, src in enumerate((colpad, bitpad)):
                        o = slot_ps[:, j * PAIRS:(j + 1) * PAIRS]
                        pe.matmul(o, src[:, SLOTS:3 * SLOTS], sel_even, start=True, stop=False)
                        ins = pe.matmul(o, src[:, 0:2 * SLOTS], sel_odd, start=False, stop=True)
                    ins.then_inc(S["slots_turned"], 1)

                def pe_batch(i, b, par):
                    pe_second(pe, i, b, par)
                    nodes.tensor(pe, i, b)

                def section(n, t, s, odd, first=False, later=False, compact=None):
                    if not (isinstance(n, int) and n < 2):
                        pe.wait_ge(section_read, n - 1)
                    for h in range(2):
                        cols = slice(h * 512, (h + 1) * 512)
                        pe.matmul(key_ps[odd][:, cols], ones_row, column_row[:, cols], start=True, stop=False)
                    for i in range(16):
                        pe.wait_ge(eq_ready, 16 * n + i + 1)
                        for h in range(2):
                            cols = slice(h * 512, (h + 1) * 512)
                            ins = pe.matmul(key_ps[odd][:, cols], cb[:, 120 - 8 * i:248 - 8 * i],
                                            eqb[:, i % EB, cols], start=False, stop=(i == 15))
                        ins.then_inc(packed, 1)
                        if i == TURN_SLOTS and compact is not None:
                            turn_slots(compact)
                        if later:
                            batches_beside(n, odd, lambda b, par: pe_first(pe, i, b, par),
                                           lambda b, par: pe_batch(i, b, par), lambda c, par: table_step(i, c, par))
                        else:
                            hidden_step(i, n, odd)
                            if not first:
                                table_step(i, n - 1, 1 - odd)
                over_sections(pe, section)
                for i in range(16):
                    if i == TURN_SLOTS:
                        turn_slots(ST - 1)
                    pe_batch(i, LAST - 2, LAST % 2)
                    pe_first(pe, i, LAST - 1, (LAST - 1) % 2)
                for i in range(16):
                    pe_batch(i, LAST - 1, (LAST - 1) % 2)
                    pe_first(pe, i, LAST, LAST % 2, key_ps[LAST % 2])
                last_batches(lambda i, b, place: pe_first(pe, i, b, b % 2, place),
                             lambda i, b, place: pe_second(pe, i, b, b % 2),
                             lambda i, t0, m, at: last_nodes.tensor(pe, i, m))
                pe.wait_ge(S["bad_ready"], 1)
                pe.matmul(work[0:1, 0:1], bad[:, 3:4], ones[:, 0:1], start=True, stop=True)\
                    .then_inc(S["flag_summed"], 1)

            @block.vector
            def _(dve):
                for t in (turned, h_turned, colpad, bitpad, lneps):
                    ins = V.memset(t[:], 0.0)
                then(ins)
                V.memset(lneps[:], LN_EPS)
                V.memset(pturned[D:D + 1, :], 1.0)
                V.memset(h_turned[D:D + 1, :], 1.0)
                then(V.memset(turned[D:D + 1, :], 1.0))
                dve.wait_ge(weights_T, 1)
                V.tensor_copy(w0a[0:D, :], work[0:D, 0:D])
                V.tensor_copy(wqk[0:D, :], work[0:D, D:3 * D])
                V.tensor_copy(par[:], work[:, 512:512 + NPAR]).then_inc(params_bc, 1)
                dve.wait_ge(params_bc, 1)
                then(V.reciprocal(att_s[:, 2:3], par[:, 3:4]))
                then(V.tensor_scalar(att_s[:, 0:1], att_s[:, 2:3], 2.0, None, ALU.mult))
                V.tensor_tensor(att_s[:, 1:2], att_s[:, 0:1], par[:, 4:5], ALU.add)
                dve.wait_ge(exps_ready, 1)
                V.tensor_copy(esc_h[:], esc[:, 0:1].to_broadcast([P, CT]))
                V.tensor_copy(esc_qk[:, :, 0], esc[:, 1:2].to_broadcast([P, CT]))
                V.tensor_copy(esc_qk[:, :, 1], esc[:, 2:3].to_broadcast([P, CT]))
                V.memset(bad[:], 0.0).then_inc(setup_done, 1)

                def ratio(st, squares, esct):
                    then(V.tensor_tensor(st[:, 3, :], st[:, 2, :], esct, ALU.mult))
                    reduce_x(st[:, 6, :], squares[:, :, 1:D])
                    then(V.tensor_scalar(st[:, 3, :], st[:, 3, :], 1.1, None, ALU.add))
                    V.tensor_scalar(st[:, 6, :], st[:, 6, :], 1e-8, None, ALU.max)
                    then(V.tensor_tensor(st[:, 4, :], st[:, 3, :], st[:, 3, :], ALU.mult))
                    V.reciprocal(st[:, 7, :], st[:, 6, :])
                    then(V.tensor_scalar(st[:, 4, :], st[:, 4, :], -1.0, None, ALU.add))
                    return V.tensor_tensor(st[:, 4, :], st[:, 4, :], st[:, 7, :], ALU.mult)

                def hidden_step(i, c, par):
                    rows = xs[:, bass.ds(c * CT, CT), :]
                    early = isinstance(c, int)
                    if i == 0:
                        if early and c == 0:
                            dve.wait_ge(x_in, 16)
                        then(reduce_x(st[:, 6, :], rows))
                        then(V.tensor_scalar(st[:, 6, :], st[:, 6, :], 1.0 / D, None, ALU.mult))
                        then(V.tensor_tensor(centred[:], rows, bc(st[:, 6, :], CT), ALU.subtract))
                        if not (early and c == 0):
                            dve.wait_ge(S["nat_turned"], c)
                        then(V.tensor_tensor(nat[:], centred[:], centred[:], ALU.mult))
                        then(reduce_x(st[:, 7, :], nat[:]))
                        V.tensor_scalar(st[:, 0, :], st[:, 7, :], 1.0 / D, None, ALU.mult)\
                            .then_inc(S["var_ready"], 1)
                    if i == 3:
                        dve.wait_ge(S["std_ready"], c + 1)
                        then(V.reciprocal(st[:, 7, :], st[:, 1, :]))
                        V.tensor_tensor(nat[:], centred[:], bc(st[:, 7, :], CT), ALU.mult)\
                            .then_inc(S["nat_ready"], 1)
                    if i == 9:
                        dve.wait_ge(S["gate_ready"], c + 1)
                        ratio(st, centred, esc_h[:]).then_inc(S["ratio_ready"], 1)
                    if i == 12:
                        dve.wait_ge(S["root_ready"], c + 1)
                        if not (early and c < 2):
                            dve.wait_ge(S["table_written"], 16 * c - 16)
                        V.tensor_tensor(kh_of[par][:, :, D + 1:2 * D],
                                        slot_ps.rearrange("p (t d) -> p t d", d=D)[:, :, 1:D],
                                        st[:, 5, :].unsqueeze(2).to_broadcast([P, CT, D - 1]), ALU.mult)
                        V.tensor_copy(kh_of[par][:, :, D], st[:, 3, :]).then_inc(S["h_ready"], 1)

                def table_step(i, c, par):
                    if i == 10:
                        dve.wait_ge(S["qk_gate_ready"], c + 1)
                        ratio(stqk, sqr, esc_qk[:].rearrange("p a b -> p (a b)")).then_inc(S["qk_ratio_ready"], 1)
                    if i == 13:
                        dve.wait_ge(S["qk_root_ready"], c + 1)
                        root = stqk[:, 5, :].unsqueeze(2).to_broadcast([P, 2 * CT, D - 1])
                        qk = work[:].rearrange("p (t d) -> p t d", d=D)
                        time = stqk[:, 3, :]
                        V.tensor_tensor(q_rows[:, :, 1:D], qk[:, 0:2 * CT:2, 1:D], root[:, 0:2 * CT:2, :], ALU.mult)
                        V.tensor_tensor(kh_of[par][:, :, 1:D], qk[:, 1:2 * CT:2, 1:D], root[:, 1:2 * CT:2, :],
                                        ALU.mult)
                        V.tensor_copy(kh_of[par][:, :, 0], time[:, 1:2 * CT:2])
                        V.tensor_scalar(q_rows[:, :, 0], time[:, 0:2 * CT:2], -1.0, None, ALU.mult)\
                            .then_inc(S["q_ready"], 1)

                def read_section(n, s, odd):
                    for u in range(NSUB):
                        ins = V.max(best[:, odd, 8 * u:8 * u + 8], key_ps[odd][:, SUB * u:SUB * (u + 1)])
                    ins.then_inc(section_read, 1)
                    dve.wait_ge(section_read, n + 1)
                    then(V.tensor_copy(cand[:, bass.ds(s * (NSUB * 8), NSUB * 8)], best[:, odd, :]))

                def compact_step(i, t):
                    if i == EB:
                        V.tensor_reduce(over[:, bass.ds(2 * t, 1)], cand[:, 7:NS * NSUB * 8:8], AX.X, ALU.max)
                    if EB <= i < EB + SLOTS // 8:
                        e = slice(8 * (i - EB), 8 * (i - EB) + 8)
                        then(V.max(key8[:, e], cand[:]))
                        then(V.max_index(pos8[:, e], key8[:, e], cand[:]))
                        then(V.match_replace(cand[:], key8[:, e], cand[:], -1.0))
                    if i == TURN_SLOTS - 1:
                        V.tensor_copy(over[:, bass.ds(2 * t + 1, 1)], key8[:, SLOTS - 1:SLOTS])
                        then(V.tensor_copy(keyi[:], key8[:]))
                        V.tensor_scalar(lowi[:], keyi[:], SUB - 1, None, ALU.bitwise_and)
                        then(V.tensor_scalar(pos8[:], pos8[:], 3, SUBBITS, ALU.logical_shift_right,
                                             ALU.logical_shift_left))
                        then(V.tensor_scalar(keyi[:], keyi[:], SUBBITS, None, ALU.logical_shift_right))
                        V.tensor_tensor(colpad[:, SLOTS:2 * SLOTS], lowi[:], pos8[:].bitcast(I32), ALU.add)
                        V.tensor_copy(bitpad[:, SLOTS:2 * SLOTS], keyi[:]).then_inc(S["slots_ready"], 1)
                    half = PAIRS // 2
                    bits = wide_a[:].bitcast(I32)
                    if i == TURN_SLOTS + 1:
                        dve.wait_ge(S["slots_turned"], t + 1)
                        V.tensor_copy(biti[:], slot_ps[:, PAIRS:2 * PAIRS])
                        then(V.tensor_copy(columns[:, bass.ds(t * PAIRS, PAIRS)], slot_ps[:, 0:PAIRS]))
                    if i in (TURN_SLOTS + 1, TURN_SLOTS + 2):
                        h = i - TURN_SLOTS - 1
                        then(V.tensor_tensor(
                            bits.rearrange("p (c r) -> p c r", r=32),
                            biti[:, h * half:(h + 1) * half].unsqueeze(2).to_broadcast([P, half, 32]),
                            ci[:].unsqueeze(1).to_broadcast([P, half, 32]), ALU.bitwise_and))
                        ins = V.tensor_scalar(mask[:, bass.ds(t * (PAIRS * 32) + h * half * 32, half * 32)], bits,
                                              1.0, None, ALU.min)
                        if h == 0:
                            then(ins)
                        else:
                            ins.then_inc(S["columns_ready"], 1)

                def dve_batch(i, b, t0, par):
                    dve_second(dve, i, b, support[:, par, :, :])
                    nodes.vector(dve, i, t0, b, support[:, par, :, :])

                def section(n, t, s, odd, first=False, later=False, compact=None):
                    for i in range(16):
                        slot, e = (16 * odd + i) % RING, i % EB
                        dve.wait_ge(adj_in[slot], 16 * n + 16)
                        if not (first and i < EB):
                            dve.wait_ge(packed, 16 * n + (i - EB + 1))
                        V.tensor_scalar(eqb[:, e, :], ring[:, slot, :], 1.0, None, ALU.is_equal)\
                            .then_inc(eq_ready, 1)
                        if i == EB - 1 and not first:
                            read_section(n - 1, s - 1 if compact is None else NS - 1, 1 - odd)
                        if compact is not None:
                            compact_step(i, compact)
                        if later:
                            batches_beside(n, odd, lambda b, par: None,
                                           lambda b, par: dve_batch(i, b, n * TB - (NS + 2) * TB, par),
                                           lambda c, par: table_step(i, c, par))
                        else:
                            hidden_step(i, n, odd)
                            if not first:
                                table_step(i, n - 1, 1 - odd)
                over_sections(dve, section, [(step, *DVE_STEPS[0:2])])
                for i in range(16):
                    if i == EB - 1:
                        dve.wait_ge(packed, 16 * SECT)
                        read_section(SECT - 1, NS - 1, 1)
                    compact_step(i, ST - 1)
                    dve_batch(i, LAST - 2, (LAST - 2) * TB, LAST % 2)
                for i in range(16):
                    dve_batch(i, LAST - 1, (LAST - 1) * TB, (LAST - 1) % 2)
                dve.wait_ge(row_summed, 16 * SECT)
                then(V.memset(last_nodes.turned[D:D + 1, :], 1.0))
                last_batches(lambda i, b, place: None,
                             lambda i, b, place: dve_second(dve, i, b, last_support[:, (b - LAST) * TB:(b - LAST + 1) * TB, :]),
                             lambda i, t0, m, at: last_nodes.vector(dve, i, t0, m, last_support[:, at:at + GROUP, :]))
                dve.wait_ge(S["y_ready"], POSTS)
                V.tensor_reduce(bad[:, 0:1], over[:], AX.X, ALU.max)
                then(V.tensor_reduce(total[:].rearrange("p (t i) -> p t i", i=16),
                                     rowsum[:].rearrange("p (t s i) -> p t i s", s=NS, i=16), AX.X, ALU.add))
                V.tensor_scalar(bad[:, 1:2], bad[:, 0:1], float(SUB), None, ALU.is_ge)
                then(V.tensor_tensor(total[:], total[:], deg[:], ALU.not_equal))
                then(V.tensor_reduce(bad[:, 2:3], total[:], AX.X, ALU.max))
                V.tensor_tensor(bad[:, 3:4], bad[:, 1:2], bad[:, 2:3], ALU.max).then_inc(S["bad_ready"], 1)
                dve.wait_ge(S["flag_summed"], 1)
                V.tensor_scalar(flag[:], work[0:1, 0:1], 1.0, None, ALU.min).then_inc(S["flag_ready"], 1)

            @block.gpsimd
            def _(pool):
                pool.wait_ge(S["table_written"], 16 * NC)

                for b in range(NB):
                    if b % BPS == 0:
                        pool.wait_ge(S["columns_ready"], b // BPS + 1)
                    if b >= 2:
                        pool.wait_ge(S["support_ready"], b - 1)
                    for q in range(PB):
                        column = columns[:, b * PB + q:b * PB + q + 1]
                        nc.gpsimd.indirect_dma_start(gat[:, b % 2, q, :], None, table[:, :],
                                                     bass.IndirectOffsetOnAxis(column, 0))\
                            .then_inc(gathered[b % 2], 16)

        def flagged(eng):
            return eng.value_load(flag[0:1, 0:1], min_val=0, max_val=1)

        class Dense:

            def __init__(self, tag, attention):
                self.attention = attention
                self.T = {k: sem(f"{tag}_{k}") for k in
                          ("rows_in", "x_in", "keys_turned", "keys_copied", "query_ready", "scores_ready",
                           "gate_ready", "weights_ready", "turned", "copied", "product_ready", "added")}
                self.block_in = [sem(f"{tag}_block_in_{i}") for i in range(2)]
                self.count = Count(sem(f"{tag}_dve_step"))

            def over_blocks(self, eng, before, body, count=None, per=0):
                with eng.Fori(0, N // SEC) as c:
                    with ExitStack() as outer:
                        if count:
                            outer.enter_context(count.loop(c, N // SEC, per * NT // 2))
                        before(c)
                        with eng.Fori(0, NT // 2) as k:
                            with ExitStack() as inner:
                                if count:
                                    inner.enter_context(count.loop(k, NT // 2, per))
                                for odd in range(2):
                                    body(c, 2 * k + odd, NT * c + 2 * k + odd, odd)

            def sync(self, sp):
                T = self.T
                if self.attention:
                    sp.dma_start(xs[:], x_t).then_inc(T["x_in"], 16)

                def load_rows(c):
                    sp.wait_ge(T["added"], NT * c + 2)
                    if self.attention:
                        src, dst = table_t[:, bass.ds(c * CT, CT), :], kh
                    else:
                        src, dst = ytable_t[:, bass.ds(c * CT, CT), :], kh[:, :, D:2 * D]
                    sp.dma_start(dst, src).then_inc(T["rows_in"], 16)

                def load_block(c, t, m, odd):
                    sp.wait_ge(T["added"], m + 1)
                    sp.dma_start(ring[:, odd, :], adj_t[t, :, bass.ds(c * SEC, SEC)]).then_inc(self.block_in[odd], 16)
                self.over_blocks(sp, load_rows, load_block)

            def tensor(self, pe):
                T = self.T

                def turn_keys(c):
                    if self.attention:
                        pe.wait_ge(T["rows_in"], 16 * c + 16)
                        for u in range(CT):
                            if u == 0:
                                ins = pe.matmul(work[0:D, 0:P], kh[:, u, 0:D], ident, start=True, stop=True)
                            else:
                                ins = pe.transpose(work[0:D, u * P:(u + 1) * P], kh[:, u, 0:D], ident)
                        ins.then_inc(T["keys_turned"], 1)

                def multiply(c, t, m, odd):
                    src = ring[:, odd, :]
                    if self.attention:
                        src = wide_a[:]
                        pe.wait_ge(T["keys_copied"], c + 1)
                        pe.wait_ge(T["query_ready"], m + 1)
                        for h in range(2):
                            ins = pe.matmul(key_ps[1][:, h * 512:(h + 1) * 512], att[0:D, 0:P],
                                            turned[0:D, h * 512:(h + 1) * 512], start=True, stop=True)
                        ins.then_inc(T["scores_ready"], 1)
                        pe.wait_ge(T["weights_ready"], m + 1)
                    else:
                        pe.wait_ge(self.block_in[odd], (m - odd) * 8 + 16)
                    for u in range(CT):
                        ins = pe.transpose(key_ps[0][:, u * P:(u + 1) * P], src[:, u * P:(u + 1) * P], ident)
                    ins.then_inc(T["turned"], 1)
                    pe.wait_ge(T["rows_in"], 16 * c + 16)
                    pe.wait_ge(T["copied"], m + 1)
                    for u in range(CT):
                        ins = pe.matmul(work[:, 0:D], wide[:, u * P:(u + 1) * P], kh[:, u, D:2 * D],
                                        start=(u == 0), stop=(u == CT - 1))
                    ins.then_inc(T["product_ready"], 1)
                    pe.wait_ge(T["added"], m + 3)
                self.over_blocks(pe, turn_keys, multiply)

            def scalar(self, act):
                T = self.T

                def copy_keys(c):
                    if self.attention:
                        act.wait_ge(T["keys_turned"], c + 1)
                        act.activation(turned[0:D, :], work[0:D, :], ACT.Copy).then_inc(T["keys_copied"], 1)

                def gate_block(c, t, m, odd):
                    if self.attention:
                        act.activation(att[0:D, 0:P], qT[:, bass.ds(t * P, P)], ACT.Copy)\
                            .then_inc(T["query_ready"], 1)
                        act.wait_ge(T["scores_ready"], m + 1)
                        act.activation(wide_a[:], key_ps[1][:], ACT.Sigmoid, bias=att_s[:, 1:2],
                                       scale=att_s[:, 0:1]).then_inc(T["gate_ready"], 1)
                    act.wait_ge(T["turned"], m + 1)
                    act.activation(wide, key_ps[0][:], ACT.Copy).then_inc(T["copied"], 1)
                self.over_blocks(act, copy_keys, gate_block)

            def vector(self, dve):
                T, count = self.T, self.count
                if self.attention:
                    V.memset(deg[:], 0.0)
                V.memset(agg[:], 0.0).then_inc(T["added"], 1)
                V.memset(bad[:, 0:1], 0.0).then_inc(T["added"], 1)

                def add_block(c, t, m, odd):
                    if self.attention:
                        dve.wait_ge(self.block_in[odd], (m - odd) * 8 + 16)
                        then(reduce_x(bad[:, 1:2], ring[:, odd, :]), count)
                        V.tensor_tensor(deg[:, bass.ds(t, 1)], deg[:, bass.ds(t, 1)], bad[:, 1:2], ALU.add)
                        dve.wait_ge(T["gate_ready"], m + 1)
                        V.tensor_tensor(wide_a[:], wide_a[:], ring[:, odd, :], ALU.mult)\
                            .then_inc(T["weights_ready"], 1)
                    dve.wait_ge(T["product_ready"], m + 1)
                    V.tensor_tensor(agg[:, bass.ds(t, 1), :], agg[:, bass.ds(t, 1), :],
                                    work[:, 0:D].unsqueeze(1), ALU.add).then_inc(T["added"], 1)
                self.over_blocks(dve, lambda c: None, add_block, count, 2 * self.attention)
                dve.wait_ge(T["added"], NT * (N // SEC) + 2)

        wide = kh_of[1].rearrange("p t d -> p (t d)")
        first_layer = Dense("dense_0", True)
        with nc.Block() as block:
            @block.sync
            def _(sp):
                with sp.If(flagged(sp) > 0):
                    first_layer.sync(sp)
                    sp.nop()

            @block.tensor
            def _(pe):
                with pe.If(flagged(pe) > 0):
                    first_layer.tensor(pe)
                    with pe.Fori(0, NB) as b:
                        pe.wait_ge(S["y_ready"], b + POSTS)
                        for i in range(16):
                            nodes.tensor(pe, i, b + POSTS)
                    pe.nop()

            @block.scalar
            def _(act):
                with act.If(flagged(act) > 0):
                    first_layer.scalar(act)
                    with act.Fori(0, NB) as b:
                        for i in range(16):
                            nodes.scalar(act, i, b * TB, b + POSTS)
                    act.wait_ge(S["y_written"], 16 * (POSTS + NB))
                    act.nop()

            @block.vector
            def _(dve):
                with dve.If(flagged(dve) > 0):
                    first_layer.vector(dve)
                    dve.wait_ge(first_layer.T["x_in"], 16)
                    with dve.Fori(0, NB) as b:
                        with first_layer.count.loop(b, NB, POST_STEPS):
                            for i in range(16):
                                nodes.vector(dve, i, b * TB, b + POSTS, agg[:, bass.ds(b * TB, TB), :],
                                             first_layer.count)
                    dve.nop()

        second_layer = Dense("dense_1", False)
        names = ("mask_ready", "product_ready", "rows_done", "sum_ready", "total_ready", "centred",
                 "squares", "squares_sum", "var_ready_bn", "std_bn", "out_ready", "out_written")
        B = {k: sem(k) for k in names}
        ygathered = [sem(f"y_gathered_{i}") for i in range(2)]
        acc = psq
        flat = lambda a: a.rearrange("p t d -> p (t d)")

        with nc.Block() as block:
            @block.gpsimd
            def _(pool):
                with pool.If(flagged(pool) < 1):
                    for b in range(NB):
                        if b >= 2:
                            pool.wait_ge(B["product_ready"], b - 1)
                        for q in range(PB):
                            column = columns[:, b * PB + q:b * PB + q + 1]
                            nc.gpsimd.indirect_dma_start(ygat[:, b % 2, q, :], None, ytable[:, :],
                                                         bass.IndirectOffsetOnAxis(column, 0))\
                                .then_inc(ygathered[b % 2], 16)
                    pool.nop()

            @block.tensor
            def _(pe):
                with pe.If(flagged(pe) > 0):
                    second_layer.tensor(pe)
                    pe.nop()
                with pe.Else():
                    def product(b, odd, first=False):
                        pe.wait_ge(ygathered[odd], (b - odd) * (8 * PB) + 16 * PB)
                        pe.wait_ge(B["mask_ready"], b + 1)
                        if not first:
                            pe.wait_ge(B["rows_done"], b - 1)
                        for t in range(PB):
                            q, r = 32 * (t % 4), t // 4
                            ins = pe.matmul(work[q:q + 32, 512 * odd + r * D:512 * odd + (r + 1) * D],
                                            mstat[:, odd, t * 32:(t + 1) * 32], ygat[:, odd, t, :],
                                            start=True, stop=True, tile_position=(0, q))
                        ins.then_inc(B["product_ready"], 1)
                    product(0, 0, first=True)
                    product(1, 1, first=True)
                    with pe.Fori(1, NB // 2) as k:
                        for odd in range(2):
                            product(2 * k + odd, odd)
                    pe.nop()
                pe.wait_ge(B["sum_ready"], 1)
                pe.matmul(work[:, 0:TB * D], ones, flat(acc[:]), start=True, stop=True).then_inc(B["total_ready"], 1)
                for c in range(NC):
                    pe.wait_ge(B["squares"], c + 1)
                    ins = pe.matmul(work[:, 512:1024], ones, flat(ys[:, c * CT:(c + 1) * CT, :]),
                                    start=(c == 0), stop=(c == NC - 1))
                ins.then_inc(B["squares_sum"], 1)

            @block.scalar
            def _(act):
                with act.If(flagged(act) > 0):
                    second_layer.scalar(act)
                    act.nop()
                with act.Else():
                    def mask_of(b, odd, first=False):
                        if not first:
                            act.wait_ge(B["product_ready"], b - 1)
                        act.activation(mstat[:, odd, :], mask[:, bass.ds(b * (PB * 32), PB * 32)], ACT.Copy)\
                            .then_inc(B["mask_ready"], 1)
                    mask_of(0, 0, first=True)
                    mask_of(1, 1, first=True)
                    with act.Fori(1, NB // 2) as k:
                        for odd in range(2):
                            mask_of(2 * k + odd, odd)
                    act.nop()
                for c in range(NC):
                    r = slice(c * CT, (c + 1) * CT)
                    act.wait_ge(B["centred"], c + 1)
                    act.activation(ys[:, r, :], agg[:, r, :], ACT.Square).then_inc(B["squares"], 1)
                act.wait_ge(B["var_ready_bn"], 1)
                act.activation(bn[:, 2, :], bn[:, 1, :], ACT.Sqrt).then_inc(B["std_bn"], 1)
                act.wait_ge(B["std_bn"], 1)

            @block.vector
            def _(dve):
                then(V.memset(acc[:], 0.0))

                def rows_of(b, product, count):
                    rows = bass.ds(b * TB, TB)
                    then(V.tensor_tensor(pxc[:], product, ys[:, rows, :], ALU.add), count)
                    V.tensor_tensor(agg[:, rows, :], pxc[:], bc(dinv[:, rows], TB), ALU.mult)\
                        .then_inc(B["rows_done"], 1)
                    dve.wait_ge(B["rows_done"], b + 1)
                    then(V.tensor_tensor(acc[:], acc[:], agg[:, rows, :], ALU.add), count)
                with dve.If(flagged(dve) > 0):
                    second_layer.vector(dve)
                    with dve.Fori(0, NB) as b:
                        with second_layer.count.loop(b, NB, 2):
                            rows_of(b, agg[:, bass.ds(b * TB, TB), :], second_layer.count)
                    dve.nop()
                with dve.Else():
                    count = Count(sem("rows_step"))
                    with dve.Fori(0, NB // 2) as k:
                        with count.loop(k, NB // 2, 4):
                            for odd in range(2):
                                dve.wait_ge(B["product_ready"], 2 * k + odd + 1)
                                rows_of(2 * k + odd, work[:, 512 * odd:512 * odd + TB * D].rearrange(
                                    "p (t d) -> p t d", d=D), count)
                    dve.nop()
                V.memset(pst[:, 0, 0:1], 0.0).then_inc(B["sum_ready"], 1)
                dve.wait_ge(B["total_ready"], 1)
                then(V.tensor_copy(bn[:, 3:5, :], work[:, 0:TB * D].rearrange("p (t d) -> p t d", d=D)))
                then(V.tensor_tensor(bn[:, 0, :], bn[:, 3, :], bn[:, 4, :], ALU.add))
                then(V.tensor_scalar(bn[:, 0, :], bn[:, 0, :], 1.0 / N, None, ALU.mult))
                spread = lambda row: row.unsqueeze(1).to_broadcast([P, CT, D])
                for c in range(NC):
                    r = slice(c * CT, (c + 1) * CT)
                    V.tensor_tensor(agg[:, r, :], agg[:, r, :], spread(bn[:, 0, :]), ALU.subtract)\
                        .then_inc(B["centred"], 1)
                dve.wait_ge(B["squares_sum"], 1)
                then(V.tensor_reduce(bn[:, 5, :], work[:, 512:1024].rearrange("p (t d) -> p d t", d=D),
                                     AX.X, ALU.add))
                V.tensor_scalar(bn[:, 1, :], bn[:, 5, :], 1.0 / N, BN_EPS, ALU.mult, ALU.add)\
                    .then_inc(B["var_ready_bn"], 1)
                dve.wait_ge(B["std_bn"], 1)
                then(V.reciprocal(bn[:, 3, :], bn[:, 2, :]))
                then(V.tensor_tensor(bn[:, 4, :], bn[:, 3, :], par[:, 5:5 + D], ALU.mult))
                for c in range(NC):
                    r = slice(c * CT, (c + 1) * CT)
                    a = agg[:, r, :]
                    then(V.tensor_tensor(a, a, spread(bn[:, 4, :]), ALU.mult))
                    then(V.tensor_tensor(a, a, spread(par[:, 5 + D:5 + 2 * D]), ALU.add))
                    then(V.scalar_tensor_tensor(out=a, in0=a, scalar=SLOPE, in1=a, op0=ALU.mult, op1=ALU.max))
                    V.tensor_tensor(xs[:, r, :], xs[:, r, :], a, ALU.add).then_inc(B["out_ready"], 1)

            @block.sync
            def _(sp):
                with sp.If(flagged(sp) > 0):
                    second_layer.sync(sp)
                    sp.nop()
                for c in range(NC):
                    sp.wait_ge(B["out_ready"], c + 1)
                    sp.dma_start(out_t[:, c * CT:(c + 1) * CT, :], xs[:, c * CT:(c + 1) * CT, :])\
                        .then_inc(B["out_written"], 16)
                sp.wait_ge(B["out_written"], 16 * NC)


POST_STEPS = 13
DVE_STEPS = (30, 30, 0)

_INS = ["x", "adj", "L0_gnn_W", "L0_gnn_b", "L0_gnn_scale", "L0_gnn_Wq", "L0_gnn_bq", "L0_gnn_scale_q",
        "L0_gnn_Wk", "L0_gnn_bk", "L0_gnn_scale_k", "L0_gnn_att_bias", "L0_gnn_att_scale",
        "L1_gnn_W", "L1_gnn_b", "L1_gnn_gamma", "L1_gnn_beta"]


def kernel(**inputs):
    import numpy as np
    import concourse.bacc as bacc
    from concourse.bass_utils import run_bass_kernel_spmd

    nc = bacc.Bacc("TRN2", target_bir_lowering=False, num_devices=1)
    arrays, args = {}, []
    laid = {name: np.ascontiguousarray(inputs[name]) for name in _INS}
    for name, a in laid.items():
        if a.ndim == 0:
            laid[name] = a.reshape(1, 1)
    for name, a in {**laid, **host_constants(laid["x"].shape[0])}.items():
        arrays[f"in_{name}"] = a
        args.append(nc.dram_tensor(f"in_{name}", a.shape, mybir.dt.from_np(a.dtype), kind="ExternalInput").ap())
    out = nc.dram_tensor("out_0", laid["x"].shape, F32, kind="ExternalOutput").ap()
    graph_layers(nc, *args, out)
    r = run_bass_kernel_spmd(nc, [arrays], core_ids=[0])
    return r.results[0]["out_0"]
```

```python
from contextlib import ExitStack, contextmanager

import concourse.bass as bass
from concourse import mybir

P = 128
ALU = mybir.AluOpType
ACT = mybir.ActivationFunctionType
AX = mybir.AxisListType
F32 = mybir.dt.float32
BF16 = mybir.dt.bfloat16
I32 = mybir.dt.int32
U32 = mybir.dt.uint32
U8 = mybir.dt.uint8

GR = 16
SEC = 1024
SUB = 128
SUBBITS = 7
NSUB = SEC // SUB
SLOTS = 64
NCONST = 18
EARLY = 3
RING = 16
EB = 4
PB = 8
TB = 2
CT = 8
LN_EPS = 1e-5
BN_EPS = 1e-5
SLOPE = 0.01


class Count:

    def __init__(self, sem):
        self.sem, self.done, self.off = sem, 0, 0

    def inc(self, ins, by=1):
        ins.then_inc(self.sem, by)
        self.done += by

    def now(self):
        return self.off + self.done

    @contextmanager
    def loop(self, i, trips, per):
        outer, start = self.off, self.done
        self.off = outer + i * per
        yield
        assert self.done - start == per, (self.done - start, per)
        self.off, self.done = outer, start + trips * per


def host_constants(n):
    import numpy as np

    f = np.zeros((P, P + P + 2 * SLOTS), np.float32)
    f[:, 0:P] = np.eye(P)
    f[:, P:2 * P] = 1.0
    for c in range(SLOTS):
        f[2 * c, 2 * P + c] = 1.0
        f[2 * c + 1, 2 * P + SLOTS + c] = 1.0
    b = np.zeros((P, 248 + P + SEC), np.float32)
    for p in range(P):
        b[p, 120 + p // GR] = 2.0 ** (p % GR + SUBBITS)
    b[0, 248:248 + P] = 1.0
    b[0, 248 + P:] = np.arange(SEC) % SUB
    i = np.zeros((P, 2 * GR), np.int32)
    for p in range(P):
        h = p // SLOTS
        i[p, h * GR:(h + 1) * GR] = 2 ** np.arange(GR)
    halves = np.ascontiguousarray(b.view(np.uint16)[:, 1::2])
    return {"const_f": f, "const_b": halves, "const_i": i}


def graph_layers(nc, x, adj, W0, b0, scale0, Wq, bq, scale_q, Wk, bk, scale_k, att_bias, att_scale,
                 W1, b1, gamma, beta, const_f, const_b, const_i, out):
    N, D = x.shape
    NT = N // P
    ST = NT // 16
    NS = N // SEC
    SECT = ST * NS
    BPS = 16 // TB
    NB = ST * BPS
    PAIRS = 64
    NC = NT // CT
    LAST = NB - BPS
    assert NS == BPS == NC == 8 and D == 64

    table = nc.dram_tensor("key_and_h_table", [N, 2 * D], F32).ap()
    ytable = nc.dram_tensor("y_table", [N, D], F32).ap()
    table_t = table.rearrange("(t p) d -> p t d", p=P)
    ytable_t = ytable.rearrange("(t p) d -> p t d", p=P)
    adj_t = adj.rearrange("(t p) n -> t p n", p=P)
    x_t = x.rearrange("(t p) d -> p t d", p=P)
    out_t = out.rearrange("(t p) d -> p t d", p=P)

    with ExitStack() as ctx:
        def sb(name, shape, dt=F32):
            return ctx.enter_context(nc.sbuf_tensor(name, shape, dt))

        def sem(name):
            return ctx.enter_context(nc.semaphore(name))

        xs = sb("x_rows", [P, NT, D])
        ys = sb("y_rows", [P, NT, D])
        deg = sb("degree", [P, NT])
        dinv = sb("inv_sqrt_degree", [P, NT])
        qT = sb("q_transposed", [D, N])
        mask = sb("slot_mask", [P, ST * PAIRS * 32], U8)
        columns = sb("slot_columns", [P, ST * PAIRS], I32)
        ring = sb("adj_ring", [P, RING, SEC])
        agg = ring[:, RING // 2:RING // 2 + NT * D // SEC, :].rearrange("p a (t d) -> p (a t) d", d=D)
        eqb = sb("adj_is_one", [P, EB, SEC], BF16)
        absb = sb("adj_abs", [P, 2, SEC], BF16)
        rowsum = sb("row_sums", [P, SECT * 16])
        wide_a = sb("wide_scratch", [P, SEC])
        best = sb("best_of_subsections", [P, 2, NSUB * 8])
        cand = sb("candidates", [P, NS * NSUB * 8])
        key8 = sb("slot_keys", [P, SLOTS])
        pos8 = sb("slot_positions", [P, SLOTS], U32)
        keyi = sb("slot_keys_int", [P, SLOTS], I32)
        lowi = sb("column_in_subsection", [P, SLOTS], I32)
        colpad = sb("columns_padded", [P, 3 * SLOTS])
        bitpad = sb("bits_padded", [P, 3 * SLOTS])
        biti = sb("slot_bits", [P, PAIRS], I32)
        over = sb("overflow", [P, 2 * ST])
        total = sb("row_totals", [P, NT])
        bad = sb("bad", [P, 4])
        flag = sb("flag", [1, 1], I32)
        gat = sb("gathered", [P, 2, PB, 2 * D])
        ygat = gat[:, :, :, 0:D]
        att = sb("attention", [P, PB * 32])
        mstat = sb("batch_mask", [P, 2, PB * 32])
        attm = sb("attention_masked", [P, PB * 32])
        nat = sb("chunk_rows", [P, CT, D])
        centred = sb("chunk_centred", [P, CT, D])
        q_rows = sb("chunk_q_rows", [P, CT, D])
        kh_of = [gat[:, j, :, :] for j in range(2)]
        kh = kh_of[0]
        support = sb("batch_support", [P, 2, TB, D])
        sqr = wide_a[:].rearrange("p (t d) -> p t d", d=D)
        turned = sb("chunk_transposed", [D + 1, CT * P])
        keyT = turned[0:D, :]
        pnat = sb("batch_rows", [P, TB, D])
        psq = sb("batch_squares", [P, TB, D])
        pxc = sb("batch_centred", [P, TB, D])
        pturned = sb("batch_transposed", [D + 1, TB * P])
        pst = sb("batch_stats", [P, 6, 2 * TB])
        h_turned = sb("chunk_h_transposed", [D + 1, CT * P])
        st = sb("chunk_stats", [P, 8, CT])
        stqk = sb("chunk_stats_qk", [P, 8, 2 * CT])
        w0a = sb("w0_aug", [D + 1, D])
        wqk = sb("wqk_aug", [D + 1, 2 * D])
        w1a = sb("w1_aug", [D + 1, D])
        wnat = sb("w_natural", [D, 3, D])
        cf = sb("const_f_sb", [P, 2 * P + 2 * SLOTS])
        cb = sb("const_b_sb", [P, 248 + P + SEC], BF16)
        ci = sb("const_i_sb", [P, 2 * GR], I32)
        NPAR = 5 + 2 * D
        prow = sb("param_row", [1, NPAR])
        par = sb("params", [P, NPAR])
        esc = sb("exp_scales", [P, 3])
        esc_h = sb("exp_scale_h", [P, CT])
        esc_qk = sb("exp_scale_qk", [P, CT, 2])
        att_s = sb("att_scale_bias", [P, 4])
        bn = sb("bn_vectors", [P, 6, D])
        lneps = sb("ln_eps", [P, 1])

        key_ps = [ctx.enter_context(nc.psum_tensor(f"packed_ones_{i}", [P, SEC], F32)) for i in range(2)]
        side_ps = ctx.enter_context(nc.psum_tensor("side_work", [P, 1024], F32))
        slot_ps, post_ps = side_ps[:, 0:512], side_ps[:, 512:1024]
        work = ctx.enter_context(nc.psum_tensor("work", [P, 1024], F32))

        ident = cf[:, 0:P]
        ones = cf[:, P:2 * P]
        sel_even = cf[:, 2 * P:2 * P + SLOTS]
        sel_odd = cf[:, 2 * P + SLOTS:2 * P + 2 * SLOTS]
        ones_row = cb[:, 248:248 + P]
        column_row = cb[:, 248 + P:248 + P + SEC]

        consts_in = sem("consts_in")
        x_first_in = sem("x_first_in")
        x_in = sem("x_in")
        adj_in = [sem(f"adj_in_{i}") for i in range(RING)]
        eq_ready = sem("eq_ready")
        row_summed = sem("row_summed")
        packed = sem("packed")
        section_read = sem("section_read")
        weights_T = sem("weights_T")
        params_bc = sem("params_broadcast")
        exps_ready = sem("exps_ready")
        setup_done = sem("setup_done")
        dve_step = sem("dve_step")
        names = ("var_ready", "std_ready", "nat_ready", "nat_turned", "nat_copied", "hidden_ready",
                 "gate_ready", "ratio_ready", "root_ready", "h_ready", "h_turned", "h_copied", "qk_ready",
                 "qk_gate_ready", "qk_ratio_ready", "qk_root_ready", "q_ready", "q_turned", "q_copied",
                 "table_written", "slots_ready", "slots_turned", "columns_ready",
                 "keys_turned", "keys_copied", "scores_ready", "att_ready", "attm_ready",
                 "support_ready", "support_copied", "norm_ready", "norm_root", "x1_var", "x1_std", "x1_nat",
                 "x1_turned", "x1_copied", "xw_ready", "y_ready", "y_written", "bad_ready", "flag_summed",
                 "flag_ready")
        S = {k: sem(k) for k in names}
        gathered = [sem(f"gathered_{i}") for i in range(2)]
        last_gathered = [sem(f"last_gathered_{i}") for i in range(4)]

        def over_sections(eng, section, counters=()):
            @contextmanager
            def counted(i, trips, column):
                with ExitStack() as s:
                    for c, *per in counters:
                        s.enter_context(c.loop(i, trips, per[column]))
                    yield
            section(0, 0, 0, 0, first=True)
            section(1, 0, 1, 1)
            with eng.Fori(0, NS // 2 - 1) as k:
                with counted(k, NS // 2 - 1, 0):
                    for odd in range(2):
                        section(2 * k + 2 + odd, 0, 2 * k + 2 + odd, odd)
            for t in range(1, ST):
                for odd in range(2):
                    section(NS * t + odd, t, odd, odd, later=True, compact=(t - 1 if odd == 0 else None))
                with eng.Fori(0, NS // 2 - 1) as k:
                    with counted(k, NS // 2 - 1, 1):
                        for odd in range(2):
                            section(2 * k + NS * t + 2 + odd, t, 2 * k + 2 + odd, odd, later=True)

        def first_later(n):
            return isinstance(n, int) and n == NS

        def batches_beside(n, odd, first, second, finish):
            if first_later(n):
                finish(n - 1, 1 - odd)
                return
            if not (isinstance(n, int) and n == NS + 1):
                second(n - NS - 2, odd)
            first(n - NS - 1, 1 - odd)

        def reduce_x(dst, src, op=ALU.add):
            return nc.vector.tensor_reduce(dst, src, AX.X, op)

        def bc(col, g):
            return col.unsqueeze(2).to_broadcast([P, g, D])

        V = nc.vector
        step = Count(dve_step)

        def then(ins, count=step):
            count.inc(ins)
            nc.vector.wait_ge(count.sem, count.now())

        def turn(pe, src, c, ready, done, count=CT, dst=work):
            if ready:
                pe.wait_ge(S[ready], c + 1)
            for t in range(count):
                if t == 0:
                    pe.matmul(dst[0:D, 0:P], src(t), ident, start=True, stop=True)
                    continue
                ins = pe.transpose(dst[0:D, t * P:(t + 1) * P], src(t), ident)
            ins.then_inc(S[done], 1)

        last_gat = [gat[:, 0], gat[:, 1]] + [ring[:, j, :].rearrange("p (t d) -> p t d", d=2 * D) for j in (12, 13)]

        def rows_gathered(b, odd):
            return last_gat[(b - LAST) % 4] if isinstance(b, int) and b >= LAST else gat[:, odd]

        def pe_first(pe, i, b, odd, place=work):
            rows = rows_gathered(b, odd)
            if i == 13:
                if isinstance(b, int) and b >= LAST:
                    pe.wait_ge(last_gathered[(b - LAST) % 4], 16 * PB * (1 + (b - LAST) // 4))
                else:
                    pe.wait_ge(gathered[odd], (b - odd) * (8 * PB) + 16 * PB)
                if isinstance(b, int) and b == 0:
                    pe.wait_ge(S["q_copied"], NC)
                elif place is work:
                    pe.wait_ge(S["support_copied"], b)
                turn(pe, lambda t: rows[:, t, 0:D], b, None, "keys_turned", PB, place)
            if i == 15:
                pe.wait_ge(S["keys_copied"], b + 1)
                for t in range(PB):
                    ins = pe.matmul(place[:, t * 32:(t + 1) * 32], keyT[:, t * P:(t + 1) * P],
                                    qT[:, bass.ds(b * (PB * 32) + t * 32, 32)], start=True, stop=True)
                ins.then_inc(S["scores_ready"], 1)

        def pe_second(pe, i, b, odd):
            if i == 2:
                pe.wait_ge(S["attm_ready"], b + 1)
                for t in range(PB):
                    q, r = 32 * (t % 4), t // 4
                    pe.matmul(work[q:q + 32, 512 + r * D:512 + (r + 1) * D], attm[:, t * 32:(t + 1) * 32],
                              rows_gathered(b, odd)[:, t, D:2 * D], start=True, stop=True, tile_position=(0, q))
                    ins = pe.matmul(work[q:q + 32, 512 + TB * D + r:512 + TB * D + r + 1],
                                    mstat[:, 0, t * 32:(t + 1) * 32], ones[:, 0:1],
                                    start=True, stop=True, tile_position=(0, q))
                ins.then_inc(S["support_ready"], 1)

        def act_first(act, i, b, place=work):
            if i == 14:
                act.wait_ge(S["keys_turned"], b + 1)
                act.activation(keyT[:], place[0:D, :], ACT.Copy).then_inc(S["keys_copied"], 1)

        def act_second(act, i, b, place=work):
            if i == 0:
                act.wait_ge(S["scores_ready"], b + 1)
                act.activation(att[:], place[:, 0:PB * 32], ACT.Sigmoid, bias=att_s[:, 1:2],
                               scale=att_s[:, 0:1]).then_inc(S["att_ready"], 1)

        def dve_second(dve, i, b, dst):
            if i == 0:
                then(V.tensor_copy(mstat[:, 0, :], mask[:, bass.ds(b * (PB * 32), PB * 32)]))
            if i == 1:
                dve.wait_ge(S["att_ready"], b + 1)
                V.tensor_tensor(attm[:], att[:], mstat[:, 0, :], ALU.mult).then_inc(S["attm_ready"], 1)
            if i == 4:
                dve.wait_ge(S["support_ready"], b + 1)
                V.tensor_copy(deg[:, bass.ds(b * TB, TB)], work[:, 512 + TB * D:512 + TB * D + TB])
                V.tensor_copy(dst, work[:, 512:512 + TB * D].rearrange("p (t d) -> p t d", d=D))\
                    .then_inc(S["support_copied"], 1)
                dve.wait_ge(S["support_copied"], b + 1)

        class Nodes:

            def __init__(self, g, squares, centred, rows, turned, stats, turn_psum, product_psum):
                self.g, self.sq, self.xc, self.rows, self.turned, self.st = g, squares, centred, rows, turned, stats
                self.turn_psum, self.product_psum = turn_psum, product_psum

            def tensor(self, pe, i, m):
                if i == 9:
                    pe.wait_ge(S["x1_nat"], m + 1)
                    for t in range(self.g):
                        dst = self.turn_psum[t // 4][0:D, (t % 4) * P:(t % 4 + 1) * P]
                        if t == 0:
                            pe.matmul(dst, self.rows[:, t, :], ident, start=True, stop=True)
                            continue
                        ins = pe.transpose(dst, self.rows[:, t, :], ident)
                    ins.then_inc(S["x1_turned"], 1)
                if i == 12:
                    pe.wait_ge(S["x1_copied"], m + 1)
                    for t in range(self.g):
                        ins = pe.matmul(self.product_psum[:, t * D:(t + 1) * D],
                                        self.turned[:, t * P:(t + 1) * P], w1a[:], start=True, stop=True)
                    ins.then_inc(S["xw_ready"], 1)

            def scalar(self, act, i, t0, m):
                g, st = self.g, self.st
                if i == 5:
                    act.wait_ge(S["norm_ready"], m + 1)
                    act.activation(st[:, 1, :], st[:, 0, :], ACT.Sqrt).then_inc(S["norm_root"], 1)
                if i == 7:
                    act.wait_ge(S["x1_var"], m + 1)
                    act.activation(st[:, 3, 0:g], st[:, 2, 0:g], ACT.Sqrt, bias=lneps[:, 0:1])\
                        .then_inc(S["x1_std"], 1)
                if i == 11:
                    act.wait_ge(S["x1_turned"], m + 1)
                    for h in range(0, g, 4):
                        w = min(g, 4) * P
                        ins = act.activation(self.turned[0:D, h * P:h * P + w], self.turn_psum[h // 4][0:D, 0:w],
                                             ACT.Relu)
                    ins.then_inc(S["x1_copied"], 1)
                if i == 15:
                    act.wait_ge(S["y_ready"], m + 1)
                    act.dma_start(ytable_t[:, bass.ds(t0, g), :], ys[:, bass.ds(t0, g), :])\
                        .then_inc(S["y_written"], 16)

            def vector(self, dve, i, t0, m, src, count=step):
                g, st, sq, xc = self.g, self.st, self.sq, self.xc
                rows = bass.ds(t0, g)
                link = lambda ins: then(ins, count)
                if i == 4:
                    link(V.tensor_tensor(sq, src, src, ALU.mult))
                    V.tensor_scalar(st[:, 0, g:2 * g], deg[:, rows], 1.0, None, ALU.add)
                    link(reduce_x(st[:, 4, 0:g], sq[:, :, 1:D]))
                    link(V.tensor_tensor(st[:, 4, g:2 * g], st[:, 4, 0:g], sq[:, :, 0], ALU.subtract))
                    link(V.scalar_tensor_tensor(out=st[:, 4, 0:g], in0=st[:, 4, g:2 * g], scalar=-1.0,
                                                in1=st[:, 4, g:2 * g], op0=ALU.mult, op1=ALU.max))
                    V.tensor_scalar(st[:, 0, 0:g], st[:, 4, 0:g], 1e-8, None, ALU.max)\
                        .then_inc(S["norm_ready"], 1)
                if i == 6:
                    dve.wait_ge(S["norm_root"], m + 1)
                    link(V.reciprocal(st[:, 4, :], st[:, 1, :]))
                    V.tensor_copy(dinv[:, rows], st[:, 4, g:2 * g])
                    link(V.tensor_tensor(xc, src, bc(st[:, 4, 0:g], g), ALU.mult))
                    link(V.tensor_tensor(sq, xs[:, rows, :], xc, ALU.add))
                    reduce_x(st[:, 5, 0:g], sq)
                    link(V.tensor_copy(xs[:, rows, :], sq))
                    link(V.tensor_scalar(st[:, 5, 0:g], st[:, 5, 0:g], 1.0 / D, None, ALU.mult))
                    link(V.tensor_tensor(xc, sq, bc(st[:, 5, 0:g], g), ALU.subtract))
                    link(V.tensor_tensor(sq, xc, xc, ALU.mult))
                    link(reduce_x(st[:, 5, g:2 * g], sq))
                    V.tensor_scalar(st[:, 2, 0:g], st[:, 5, g:2 * g], 1.0 / D, None, ALU.mult)\
                        .then_inc(S["x1_var"], 1)
                if i == 8:
                    dve.wait_ge(S["x1_std"], m + 1)
                    link(V.reciprocal(st[:, 5, 0:g], st[:, 3, 0:g]))
                    V.tensor_tensor(self.rows, xc, bc(st[:, 5, 0:g], g), ALU.mult).then_inc(S["x1_nat"], 1)
                if i == 13:
                    dve.wait_ge(S["xw_ready"], m + 1)
                    V.tensor_tensor(ys[:, rows, :], self.product_psum.rearrange("p (t d) -> p t d", d=D),
                                    bc(dinv[:, rows], g), ALU.mult).then_inc(S["y_ready"], 1)

        nodes = Nodes(TB, psq[:], pxc[:], pnat[:], pturned, pst, [post_ps], post_ps[:, 0:TB * D])

        TURN_SLOTS = EB + SLOTS // 8 + 1
        GROUP = 4
        at = lambda slot, shape: ring[:, slot, 0:shape[0] * shape[1]].rearrange("p (a b) -> p a b", b=shape[1])
        last_support = at(0, (16, D))
        last_nodes = Nodes(GROUP, at(1, (GROUP, D)), at(2, (GROUP, D)), at(3, (GROUP, D)),
                           ring[0:D + 1, 4, 0:GROUP * P],
                           at(5, (6, 2 * GROUP)), [post_ps, slot_ps], work[:, 0:GROUP * D])
        POSTS = LAST + 16 // GROUP

        def last_batches(first, second, node, check=lambda: None):
            def node_steps(a, place):
                for g in range(16 // GROUP - 1):
                    steps = {(0, 1): (4, 5), (1, 0): (5, 9), (1, 1): (9, 11), (2, 0): (11, 12), (2, 1): (12, 16)}
                    for i in range(*steps.get((a - LAST - 2 * g - 1, place), (0, 0))):
                        node(i, LAST * TB + g * GROUP, LAST + g, g * GROUP)

            for a in range(LAST, NB):
                more, here, there = a + 1 < NB, key_ps[a % 2], key_ps[(a + 1) % 2]
                if more:
                    first(13, a + 1, there)
                for i in range(2):
                    second(i, a, here)
                if more:
                    first(14, a + 1, there)
                node_steps(a, 0)
                for i in range(2, 5):
                    second(i, a, here)
                if more:
                    first(15, a + 1, there)
                node_steps(a, 1)
            g = 16 // GROUP - 1
            for i in range(16):
                if i == 10:
                    check()
                node(i, LAST * TB + g * GROUP, LAST + g, g * GROUP)

        with nc.Block() as block:
            @block.sync
            def _(sp):
                small = [(cf[:], const_f), (cb[:], const_b.bitcast(BF16)), (ci[:], const_i),
                         (wnat[:, 0, :], W0), (wnat[:, 1, :], Wq), (wnat[:, 2, :], Wk), (w1a[0:D, :], W1)]
                small += [(prow[0:1, j:j + 1], s) for j, s in enumerate((scale0, scale_q, scale_k, att_scale,
                                                                        att_bias))]
                small += [(dst, src.rearrange("(a d) -> a d", a=1)) for dst, src in (
                    (w0a[D:D + 1, :], b0), (wqk[D:D + 1, 0:D], bq), (wqk[D:D + 1, D:2 * D], bk),
                    (w1a[D:D + 1, :], b1), (prow[0:1, 5:5 + D], gamma), (prow[0:1, 5 + D:5 + 2 * D], beta))]
                assert len(small) == NCONST

                def block_load(n, t, s, odd, i):
                    slot = (16 * odd + i) % RING
                    sp.dma_start(ring[:, slot, :], adj_t[16 * t + i, :, bass.ds(s * SEC, SEC)])\
                        .then_inc(adj_in[slot], 16)

                for j, (dst, src) in enumerate(small):
                    sp.dma_start(dst, src).then_inc(consts_in, 16)
                    if j % EARLY == EARLY - 1:
                        block_load(0, 0, 0, 0, j // EARLY)
                sp.dma_start(xs[:, 0:CT, :], x_t[:, 0:CT, :]).then_inc(x_first_in, 16)

                def section(n, t, s, odd, first=False, later=False, compact=None):
                    for i in range(len(small) // EARLY if first else 0, 16):
                        if not (first and i < RING):
                            sp.wait_ge(eq_ready, 16 * n + (i - RING + 1))
                            sp.wait_ge(row_summed, 16 * n + (i - RING + 1))
                        block_load(n, t, s, odd, i)
                    if first:
                        sp.dma_start(xs[:, CT:NT, :], x_t[:, CT:NT, :]).then_inc(x_in, 16)
                over_sections(sp, section)

            @block.scalar
            def _(act):
                act.wait_ge(params_bc, 1)
                act.activation(esc[:], par[:, 0:3], ACT.Exp).then_inc(exps_ready, 1)
                act.wait_ge(setup_done, 1)

                def turn_copy(c, turned_sem, copied_sem, dst):
                    act.wait_ge(S[turned_sem], c + 1)
                    act.activation(dst, work[0:D, :], ACT.Copy).then_inc(S[copied_sem], 1)

                def hidden_step(i, c):
                    if i == 2:
                        act.wait_ge(S["var_ready"], c + 1)
                        act.activation(st[:, 1, :], st[:, 0, :], ACT.Sqrt, bias=lneps[:, 0:1])\
                            .then_inc(S["std_ready"], 1)
                    if i == 5:
                        act.wait_ge(S["nat_turned"], c + 1)
                        act.activation(turned[0:D, :], side_ps[0:D, :], ACT.Relu).then_inc(S["nat_copied"], 1)
                    if i == 8:
                        act.wait_ge(S["hidden_ready"], c + 1)
                        w = slot_ps.rearrange("p (t d) -> p t d", d=D)
                        act.activation(centred[:], w, ACT.Square)
                        act.activation(st[:, 2, :], w[:, :, 0], ACT.Sigmoid).then_inc(S["gate_ready"], 1)
                    if i == 11:
                        act.wait_ge(S["ratio_ready"], c + 1)
                        act.activation(st[:, 5, :], st[:, 4, :], ACT.Sqrt).then_inc(S["root_ready"], 1)

                def table_step(i, c, par):
                    if i == 3:
                        turn_copy(c, "h_turned", "h_copied", h_turned[0:D, :])
                    if i == 8:
                        act.wait_ge(S["qk_ready"], c + 1)
                        w = work[:].rearrange("p (t d) -> p t d", d=D)
                        act.activation(sqr, w, ACT.Square)
                        act.activation(stqk[:, 2, :], w[:, :, 0], ACT.Sigmoid).then_inc(S["qk_gate_ready"], 1)
                    if i == 12:
                        act.wait_ge(S["qk_ratio_ready"], c + 1)
                        act.activation(stqk[:, 5, :], stqk[:, 4, :], ACT.Sqrt).then_inc(S["qk_root_ready"], 1)
                    if i == 14:
                        act.wait_ge(S["q_ready"], c + 1)
                        act.dma_start(table_t[:, bass.ds(c * CT, CT), :], kh_of[par])\
                            .then_inc(S["table_written"], 16)
                    if i == 15:
                        turn_copy(c, "q_turned", "q_copied", qT[:, bass.ds(c * CT * P, CT * P)])

                def act_batch(i, b, t0):
                    act_second(act, i, b)
                    nodes.scalar(act, i, t0, b)

                def section(n, t, s, odd, first=False, later=False, compact=None):
                    for i in range(16):
                        slot, e = (16 * odd + i) % RING, i % EB
                        act.wait_ge(adj_in[slot], 16 * n + 16)
                        if not (first and i < 2):
                            act.wait_ge(row_summed, 16 * n + i - 1)
                        act.activation(absb[:, i % 2, :], ring[:, slot, :], ACT.Abs,
                                       accum_out=rowsum[:, bass.ds(16 * n + i, 1)]).then_inc(row_summed, 1)
                        if later:
                            batches_beside(n, odd, lambda b, par: act_first(act, i, b),
                                           lambda b, par: act_batch(i, b, n * TB - (NS + 2) * TB),
                                           lambda c, par: table_step(i, c, par))
                        else:
                            hidden_step(i, n)
                            if not first:
                                table_step(i, n - 1, 1 - odd)
                over_sections(act, section)
                for i in range(16):
                    act_batch(i, LAST - 2, (LAST - 2) * TB)
                    act_first(act, i, LAST - 1)
                for i in range(16):
                    act_batch(i, LAST - 1, (LAST - 1) * TB)
                    act_first(act, i, LAST, key_ps[LAST % 2])
                last_batches(lambda i, b, place: act_first(act, i, b, place),
                             lambda i, b, place: act_second(act, i, b, place),
                             lambda i, t0, m, at: last_nodes.scalar(act, i, t0, m))
                act.wait_ge(S["y_written"], 16 * POSTS)

            @block.tensor
            def _(pe):
                pe.wait_ge(consts_in, 16 * NCONST)
                for j in range(3):
                    pe.transpose(work[0:D, j * D:(j + 1) * D], wnat[:, j, :], ident[0:D, 0:D])
                pe.matmul(work[:, 512:512 + NPAR], ones[0:1, :], prow[:], start=True, stop=True)\
                    .then_inc(weights_T, 1)
                pe.wait_ge(setup_done, 1)

                def hidden_step(i, c, par):
                    if i == 4:
                        turn(pe, lambda t: nat[:, t, :], c, "nat_ready", "nat_turned", dst=side_ps)
                    if i == 6:
                        pe.wait_ge(S["nat_copied"], c + 1)
                        for t in range(CT):
                            ins = pe.matmul(slot_ps[:, t * D:(t + 1) * D], turned[:, t * P:(t + 1) * P], w0a[:],
                                            start=True, stop=True)
                        ins.then_inc(S["hidden_ready"], 1)

                def table_step(i, c, par):
                    if i == 1:
                        if not (isinstance(c, int) and c == 0):
                            pe.wait_ge(S["q_copied"], c)
                        turn(pe, lambda t: kh_of[par][:, t, D:2 * D], c, "h_ready", "h_turned")
                    if i == 5:
                        pe.wait_ge(S["h_copied"], c + 1)
                        for t in range(CT):
                            ins = pe.matmul(work[:, t * 2 * D:(t + 1) * 2 * D], h_turned[:, t * P:(t + 1) * P],
                                            wqk[:], start=True, stop=True)
                        ins.then_inc(S["qk_ready"], 1)
                    if i == 14:
                        turn(pe, lambda t: q_rows[:, t, :], c, "q_ready", "q_turned")

                def turn_slots(t):
                    pe.wait_ge(S["slots_ready"], t + 1)
                    for j, src in enumerate((colpad, bitpad)):
                        o = slot_ps[:, j * PAIRS:(j + 1) * PAIRS]
                        pe.matmul(o, src[:, SLOTS:3 * SLOTS], sel_even, start=True, stop=False)
                        ins = pe.matmul(o, src[:, 0:2 * SLOTS], sel_odd, start=False, stop=True)
                    ins.then_inc(S["slots_turned"], 1)

                def pe_batch(i, b, par):
                    pe_second(pe, i, b, par)
                    nodes.tensor(pe, i, b)

                def section(n, t, s, odd, first=False, later=False, compact=None):
                    if not (isinstance(n, int) and n < 2):
                        pe.wait_ge(section_read, n - 1)
                    for h in range(2):
                        cols = slice(h * 512, (h + 1) * 512)
                        pe.matmul(key_ps[odd][:, cols], ones_row, column_row[:, cols], start=True, stop=False)
                    for i in range(16):
                        pe.wait_ge(eq_ready, 16 * n + i + 1)
                        for h in range(2):
                            cols = slice(h * 512, (h + 1) * 512)
                            ins = pe.matmul(key_ps[odd][:, cols], cb[:, 120 - 8 * i:248 - 8 * i],
                                            eqb[:, i % EB, cols], start=False, stop=(i == 15))
                        ins.then_inc(packed, 1)
                        if i == TURN_SLOTS and compact is not None:
                            turn_slots(compact)
                        if later:
                            batches_beside(n, odd, lambda b, par: pe_first(pe, i, b, par),
                                           lambda b, par: pe_batch(i, b, par), lambda c, par: table_step(i, c, par))
                        else:
                            hidden_step(i, n, odd)
                            if not first:
                                table_step(i, n - 1, 1 - odd)
                over_sections(pe, section)
                for i in range(16):
                    if i == TURN_SLOTS:
                        turn_slots(ST - 1)
                    pe_batch(i, LAST - 2, LAST % 2)
                    pe_first(pe, i, LAST - 1, (LAST - 1) % 2)
                for i in range(16):
                    pe_batch(i, LAST - 1, (LAST - 1) % 2)
                    pe_first(pe, i, LAST, LAST % 2, key_ps[LAST % 2])

                def sum_of_bad():
                    pe.wait_ge(S["bad_ready"], 1)
                    pe.matmul(work[0:1, 512:513], bad[:, 3:4], ones[:, 0:1], start=True, stop=True)\
                        .then_inc(S["flag_summed"], 1)
                last_batches(lambda i, b, place: pe_first(pe, i, b, b % 2, place),
                             lambda i, b, place: pe_second(pe, i, b, b % 2),
                             lambda i, t0, m, at: last_nodes.tensor(pe, i, m), sum_of_bad)

            @block.vector
            def _(dve):
                for t in (turned, h_turned, colpad, bitpad, lneps):
                    ins = V.memset(t[:], 0.0)
                then(ins)
                V.memset(lneps[:], LN_EPS)
                V.memset(pturned[D:D + 1, :], 1.0)
                V.memset(h_turned[D:D + 1, :], 1.0)
                then(V.memset(turned[D:D + 1, :], 1.0))
                dve.wait_ge(weights_T, 1)
                V.tensor_copy(w0a[0:D, :], work[0:D, 0:D])
                V.tensor_copy(wqk[0:D, :], work[0:D, D:3 * D])
                V.tensor_copy(par[:], work[:, 512:512 + NPAR]).then_inc(params_bc, 1)
                dve.wait_ge(params_bc, 1)
                then(V.reciprocal(att_s[:, 2:3], par[:, 3:4]))
                then(V.tensor_scalar(att_s[:, 0:1], att_s[:, 2:3], 2.0, None, ALU.mult))
                V.tensor_tensor(att_s[:, 1:2], att_s[:, 0:1], par[:, 4:5], ALU.add)
                dve.wait_ge(exps_ready, 1)
                V.tensor_copy(esc_h[:], esc[:, 0:1].to_broadcast([P, CT]))
                V.tensor_copy(esc_qk[:, :, 0], esc[:, 1:2].to_broadcast([P, CT]))
                V.tensor_copy(esc_qk[:, :, 1], esc[:, 2:3].to_broadcast([P, CT]))
                V.memset(bad[:], 0.0).then_inc(setup_done, 1)

                def ratio(st, squares, esct):
                    then(V.tensor_tensor(st[:, 3, :], st[:, 2, :], esct, ALU.mult))
                    reduce_x(st[:, 6, :], squares[:, :, 1:D])
                    then(V.tensor_scalar(st[:, 3, :], st[:, 3, :], 1.1, None, ALU.add))
                    V.tensor_scalar(st[:, 6, :], st[:, 6, :], 1e-8, None, ALU.max)
                    then(V.tensor_tensor(st[:, 4, :], st[:, 3, :], st[:, 3, :], ALU.mult))
                    V.reciprocal(st[:, 7, :], st[:, 6, :])
                    then(V.tensor_scalar(st[:, 4, :], st[:, 4, :], -1.0, None, ALU.add))
                    return V.tensor_tensor(st[:, 4, :], st[:, 4, :], st[:, 7, :], ALU.mult)

                def hidden_step(i, c, par):
                    rows = xs[:, bass.ds(c * CT, CT), :]
                    early = isinstance(c, int)
                    if i == 0:
                        if early and c < 2:
                            dve.wait_ge(x_in if c else x_first_in, 16)
                        then(reduce_x(st[:, 6, :], rows))
                        then(V.tensor_scalar(st[:, 6, :], st[:, 6, :], 1.0 / D, None, ALU.mult))
                        then(V.tensor_tensor(centred[:], rows, bc(st[:, 6, :], CT), ALU.subtract))
                        if not (early and c == 0):
                            dve.wait_ge(S["nat_turned"], c)
                        then(V.tensor_tensor(nat[:], centred[:], centred[:], ALU.mult))
                        then(reduce_x(st[:, 7, :], nat[:]))
                        V.tensor_scalar(st[:, 0, :], st[:, 7, :], 1.0 / D, None, ALU.mult)\
                            .then_inc(S["var_ready"], 1)
                    if i == 3:
                        dve.wait_ge(S["std_ready"], c + 1)
                        then(V.reciprocal(st[:, 7, :], st[:, 1, :]))
                        V.tensor_tensor(nat[:], centred[:], bc(st[:, 7, :], CT), ALU.mult)\
                            .then_inc(S["nat_ready"], 1)
                    if i == 9:
                        dve.wait_ge(S["gate_ready"], c + 1)
                        ratio(st, centred, esc_h[:]).then_inc(S["ratio_ready"], 1)
                    if i == 12:
                        dve.wait_ge(S["root_ready"], c + 1)
                        if not (early and c < 2):
                            dve.wait_ge(S["table_written"], 16 * c - 16)
                        V.tensor_tensor(kh_of[par][:, :, D + 1:2 * D],
                                        slot_ps.rearrange("p (t d) -> p t d", d=D)[:, :, 1:D],
                                        st[:, 5, :].unsqueeze(2).to_broadcast([P, CT, D - 1]), ALU.mult)
                        V.tensor_copy(kh_of[par][:, :, D], st[:, 3, :]).then_inc(S["h_ready"], 1)

                def table_step(i, c, par):
                    if i == 10:
                        dve.wait_ge(S["qk_gate_ready"], c + 1)
                        ratio(stqk, sqr, esc_qk[:].rearrange("p a b -> p (a b)")).then_inc(S["qk_ratio_ready"], 1)
                    if i == 13:
                        dve.wait_ge(S["qk_root_ready"], c + 1)
                        root = stqk[:, 5, :].unsqueeze(2).to_broadcast([P, 2 * CT, D - 1])
                        qk = work[:].rearrange("p (t d) -> p t d", d=D)
                        time = stqk[:, 3, :]
                        V.tensor_tensor(q_rows[:, :, 1:D], qk[:, 0:2 * CT:2, 1:D], root[:, 0:2 * CT:2, :], ALU.mult)
                        V.tensor_tensor(kh_of[par][:, :, 1:D], qk[:, 1:2 * CT:2, 1:D], root[:, 1:2 * CT:2, :],
                                        ALU.mult)
                        V.tensor_copy(kh_of[par][:, :, 0], time[:, 1:2 * CT:2])
                        V.tensor_scalar(q_rows[:, :, 0], time[:, 0:2 * CT:2], -1.0, None, ALU.mult)\
                            .then_inc(S["q_ready"], 1)

                def read_section(n, s, odd):
                    for u in range(NSUB):
                        ins = V.max(best[:, odd, 8 * u:8 * u + 8], key_ps[odd][:, SUB * u:SUB * (u + 1)])
                    ins.then_inc(section_read, 1)
                    dve.wait_ge(section_read, n + 1)
                    then(V.tensor_copy(cand[:, bass.ds(s * (NSUB * 8), NSUB * 8)], best[:, odd, :]))

                def compact_step(i, t):
                    if i == EB:
                        V.tensor_reduce(over[:, bass.ds(2 * t, 1)], cand[:, 7:NS * NSUB * 8:8], AX.X, ALU.max)
                    if EB <= i < EB + SLOTS // 8:
                        e = slice(8 * (i - EB), 8 * (i - EB) + 8)
                        then(V.max(key8[:, e], cand[:]))
                        then(V.max_index(pos8[:, e], key8[:, e], cand[:]))
                        then(V.match_replace(cand[:], key8[:, e], cand[:], -1.0))
                    if i == TURN_SLOTS - 1:
                        V.tensor_copy(over[:, bass.ds(2 * t + 1, 1)], key8[:, SLOTS - 1:SLOTS])
                        then(V.tensor_copy(keyi[:], key8[:]))
                        V.tensor_scalar(lowi[:], keyi[:], SUB - 1, None, ALU.bitwise_and)
                        then(V.tensor_scalar(pos8[:], pos8[:], 3, SUBBITS, ALU.logical_shift_right,
                                             ALU.logical_shift_left))
                        then(V.tensor_scalar(keyi[:], keyi[:], SUBBITS, None, ALU.logical_shift_right))
                        V.tensor_tensor(colpad[:, SLOTS:2 * SLOTS], lowi[:], pos8[:].bitcast(I32), ALU.add)
                        V.tensor_copy(bitpad[:, SLOTS:2 * SLOTS], keyi[:]).then_inc(S["slots_ready"], 1)
                    half = PAIRS // 2
                    bits = wide_a[:].bitcast(I32)
                    if i == TURN_SLOTS + 1:
                        dve.wait_ge(S["slots_turned"], t + 1)
                        V.tensor_copy(biti[:], slot_ps[:, PAIRS:2 * PAIRS])
                        V.tensor_copy(columns[:, bass.ds(t * PAIRS, PAIRS)], slot_ps[:, 0:PAIRS])\
                            .then_inc(S["columns_ready"], 1)
                        dve.wait_ge(S["columns_ready"], t + 1)
                    if i in (TURN_SLOTS + 1, TURN_SLOTS + 2):
                        h = i - TURN_SLOTS - 1
                        then(V.tensor_tensor(
                            bits.rearrange("p (c r) -> p c r", r=32),
                            biti[:, h * half:(h + 1) * half].unsqueeze(2).to_broadcast([P, half, 32]),
                            ci[:].unsqueeze(1).to_broadcast([P, half, 32]), ALU.bitwise_and))
                        ins = V.tensor_scalar(mask[:, bass.ds(t * (PAIRS * 32) + h * half * 32, half * 32)], bits,
                                              1.0, None, ALU.min)
                        then(ins)

                def dve_batch(i, b, t0, par):
                    dve_second(dve, i, b, support[:, par, :, :])
                    nodes.vector(dve, i, t0, b, support[:, par, :, :])

                def section(n, t, s, odd, first=False, later=False, compact=None):
                    for i in range(16):
                        slot, e = (16 * odd + i) % RING, i % EB
                        dve.wait_ge(adj_in[slot], 16 * n + 16)
                        if not (first and i < EB):
                            dve.wait_ge(packed, 16 * n + (i - EB + 1))
                        V.tensor_scalar(eqb[:, e, :], ring[:, slot, :], 1.0, None, ALU.is_equal)\
                            .then_inc(eq_ready, 1)
                        if i == EB - 1 and not first:
                            read_section(n - 1, s - 1 if compact is None else NS - 1, 1 - odd)
                        if compact is not None:
                            compact_step(i, compact)
                        if later:
                            batches_beside(n, odd, lambda b, par: None,
                                           lambda b, par: dve_batch(i, b, n * TB - (NS + 2) * TB, par),
                                           lambda c, par: table_step(i, c, par))
                        else:
                            hidden_step(i, n, odd)
                            if not first:
                                table_step(i, n - 1, 1 - odd)
                over_sections(dve, section, [(step, *DVE_STEPS[0:2])])
                for i in range(16):
                    if i == EB - 1:
                        dve.wait_ge(packed, 16 * SECT)
                        read_section(SECT - 1, NS - 1, 1)
                    compact_step(i, ST - 1)
                    dve_batch(i, LAST - 2, (LAST - 2) * TB, LAST % 2)
                for i in range(16):
                    dve_batch(i, LAST - 1, (LAST - 1) * TB, (LAST - 1) % 2)
                dve.wait_ge(row_summed, 16 * SECT)
                then(V.memset(last_nodes.turned[D:D + 1, :], 1.0))

                def set_flag():
                    V.tensor_reduce(bad[:, 0:1], over[:], AX.X, ALU.max)
                    then(V.tensor_reduce(total[:].rearrange("p (t i) -> p t i", i=16),
                                         rowsum[:].rearrange("p (t s i) -> p t i s", s=NS, i=16), AX.X, ALU.add))
                    V.tensor_scalar(bad[:, 1:2], bad[:, 0:1], float(SUB), None, ALU.is_ge)
                    then(V.tensor_tensor(total[:], total[:], deg[:], ALU.not_equal))
                    then(V.tensor_reduce(bad[:, 2:3], total[:], AX.X, ALU.max))
                    V.tensor_tensor(bad[:, 3:4], bad[:, 1:2], bad[:, 2:3], ALU.max).then_inc(S["bad_ready"], 1)
                    dve.wait_ge(S["flag_summed"], 1)
                    V.tensor_scalar(flag[:], work[0:1, 512:513], 1.0, None, ALU.min).then_inc(S["flag_ready"], 1)
                last_batches(lambda i, b, place: None,
                             lambda i, b, place: dve_second(
                                 dve, i, b, last_support[:, (b - LAST) * TB:(b - LAST + 1) * TB, :]),
                             lambda i, t0, m, at: last_nodes.vector(dve, i, t0, m, last_support[:, at:at + GROUP, :]),
                             set_flag)

            @block.gpsimd
            def _(pool):
                pool.wait_ge(S["table_written"], 16 * NC)

                for b in range(NB):
                    if b % BPS == 0:
                        pool.wait_ge(S["columns_ready"], b // BPS + 1)
                    last = b - LAST
                    if last in (2, 3):
                        pool.wait_ge(eq_ready, 16 * SECT)
                        pool.wait_ge(row_summed, 16 * SECT)
                    elif last >= 4:
                        pool.wait_ge(S["support_ready"], b - 3)
                    elif b >= 2:
                        pool.wait_ge(S["support_ready"], b - 1)
                    into, arrived = ((rows_gathered(b, b % 2), last_gathered[last % 4]) if last >= 0
                                     else (gat[:, b % 2], gathered[b % 2]))
                    for q in range(PB):
                        column = columns[:, b * PB + q:b * PB + q + 1]
                        nc.gpsimd.indirect_dma_start(into[:, q, :], None, table[:, :],
                                                     bass.IndirectOffsetOnAxis(column, 0))\
                            .then_inc(arrived, 16)

        def flagged(eng):
            return eng.value_load(flag[0:1, 0:1], min_val=0, max_val=1)

        class Dense:

            def __init__(self, tag, attention):
                self.attention = attention
                self.T = {k: sem(f"{tag}_{k}") for k in
                          ("rows_in", "x_in", "keys_turned", "keys_copied", "query_ready", "scores_ready",
                           "gate_ready", "weights_ready", "turned", "copied", "product_ready", "added")}
                self.block_in = [sem(f"{tag}_block_in_{i}") for i in range(2)]
                self.count = Count(sem(f"{tag}_dve_step"))

            def over_blocks(self, eng, before, body, count=None, per=0):
                with eng.Fori(0, N // SEC) as c:
                    with ExitStack() as outer:
                        if count:
                            outer.enter_context(count.loop(c, N // SEC, per * NT // 2))
                        before(c)
                        with eng.Fori(0, NT // 2) as k:
                            with ExitStack() as inner:
                                if count:
                                    inner.enter_context(count.loop(k, NT // 2, per))
                                for odd in range(2):
                                    body(c, 2 * k + odd, NT * c + 2 * k + odd, odd)

            def sync(self, sp):
                T = self.T
                if self.attention:
                    sp.dma_start(xs[:], x_t).then_inc(T["x_in"], 16)

                def load_rows(c):
                    sp.wait_ge(T["added"], NT * c + 2)
                    if self.attention:
                        src, dst = table_t[:, bass.ds(c * CT, CT), :], kh
                    else:
                        src, dst = ytable_t[:, bass.ds(c * CT, CT), :], kh[:, :, D:2 * D]
                    sp.dma_start(dst, src).then_inc(T["rows_in"], 16)

                def load_block(c, t, m, odd):
                    sp.wait_ge(T["added"], m + 1)
                    sp.dma_start(ring[:, odd, :], adj_t[t, :, bass.ds(c * SEC, SEC)]).then_inc(self.block_in[odd], 16)
                self.over_blocks(sp, load_rows, load_block)

            def tensor(self, pe):
                T = self.T

                def turn_keys(c):
                    if self.attention:
                        pe.wait_ge(T["rows_in"], 16 * c + 16)
                        for u in range(CT):
                            if u == 0:
                                ins = pe.matmul(work[0:D, 0:P], kh[:, u, 0:D], ident, start=True, stop=True)
                            else:
                                ins = pe.transpose(work[0:D, u * P:(u + 1) * P], kh[:, u, 0:D], ident)
                        ins.then_inc(T["keys_turned"], 1)

                def multiply(c, t, m, odd):
                    src = ring[:, odd, :]
                    if self.attention:
                        src = wide_a[:]
                        pe.wait_ge(T["keys_copied"], c + 1)
                        pe.wait_ge(T["query_ready"], m + 1)
                        for h in range(2):
                            ins = pe.matmul(key_ps[1][:, h * 512:(h + 1) * 512], att[0:D, 0:P],
                                            turned[0:D, h * 512:(h + 1) * 512], start=True, stop=True)
                        ins.then_inc(T["scores_ready"], 1)
                        pe.wait_ge(T["weights_ready"], m + 1)
                    else:
                        pe.wait_ge(self.block_in[odd], (m - odd) * 8 + 16)
                    for u in range(CT):
                        ins = pe.transpose(key_ps[0][:, u * P:(u + 1) * P], src[:, u * P:(u + 1) * P], ident)
                    ins.then_inc(T["turned"], 1)
                    pe.wait_ge(T["rows_in"], 16 * c + 16)
                    pe.wait_ge(T["copied"], m + 1)
                    for u in range(CT):
                        ins = pe.matmul(work[:, 0:D], wide[:, u * P:(u + 1) * P], kh[:, u, D:2 * D],
                                        start=(u == 0), stop=(u == CT - 1))
                    ins.then_inc(T["product_ready"], 1)
                    pe.wait_ge(T["added"], m + 3)
                self.over_blocks(pe, turn_keys, multiply)

            def scalar(self, act):
                T = self.T

                def copy_keys(c):
                    if self.attention:
                        act.wait_ge(T["keys_turned"], c + 1)
                        act.activation(turned[0:D, :], work[0:D, :], ACT.Copy).then_inc(T["keys_copied"], 1)

                def gate_block(c, t, m, odd):
                    if self.attention:
                        act.activation(att[0:D, 0:P], qT[:, bass.ds(t * P, P)], ACT.Copy)\
                            .then_inc(T["query_ready"], 1)
                        act.wait_ge(T["scores_ready"], m + 1)
                        act.activation(wide_a[:], key_ps[1][:], ACT.Sigmoid, bias=att_s[:, 1:2],
                                       scale=att_s[:, 0:1]).then_inc(T["gate_ready"], 1)
                    act.wait_ge(T["turned"], m + 1)
                    act.activation(wide, key_ps[0][:], ACT.Copy).then_inc(T["copied"], 1)
                self.over_blocks(act, copy_keys, gate_block)

            def vector(self, dve):
                T, count = self.T, self.count
                if self.attention:
                    V.memset(deg[:], 0.0)
                V.memset(agg[:], 0.0).then_inc(T["added"], 1)
                V.memset(bad[:, 0:1], 0.0).then_inc(T["added"], 1)

                def add_block(c, t, m, odd):
                    if self.attention:
                        dve.wait_ge(self.block_in[odd], (m - odd) * 8 + 16)
                        then(reduce_x(bad[:, 1:2], ring[:, odd, :]), count)
                        V.tensor_tensor(deg[:, bass.ds(t, 1)], deg[:, bass.ds(t, 1)], bad[:, 1:2], ALU.add)
                        dve.wait_ge(T["gate_ready"], m + 1)
                        V.tensor_tensor(wide_a[:], wide_a[:], ring[:, odd, :], ALU.mult)\
                            .then_inc(T["weights_ready"], 1)
                    dve.wait_ge(T["product_ready"], m + 1)
                    V.tensor_tensor(agg[:, bass.ds(t, 1), :], agg[:, bass.ds(t, 1), :],
                                    work[:, 0:D].unsqueeze(1), ALU.add).then_inc(T["added"], 1)
                self.over_blocks(dve, lambda c: None, add_block, count, 2 * self.attention)
                dve.wait_ge(T["added"], NT * (N // SEC) + 2)

        wide = kh_of[1].rearrange("p t d -> p (t d)")
        first_layer = Dense("dense_0", True)
        with nc.Block() as block:
            @block.sync
            def _(sp):
                with sp.If(flagged(sp) > 0):
                    first_layer.sync(sp)
                    sp.nop()

            @block.tensor
            def _(pe):
                with pe.If(flagged(pe) > 0):
                    first_layer.tensor(pe)
                    with pe.Fori(0, NB) as b:
                        pe.wait_ge(S["y_ready"], b + POSTS)
                        for i in range(16):
                            nodes.tensor(pe, i, b + POSTS)
                    pe.nop()

            @block.scalar
            def _(act):
                with act.If(flagged(act) > 0):
                    first_layer.scalar(act)
                    with act.Fori(0, NB) as b:
                        for i in range(16):
                            nodes.scalar(act, i, b * TB, b + POSTS)
                    act.wait_ge(S["y_written"], 16 * (POSTS + NB))
                    act.nop()

            @block.vector
            def _(dve):
                with dve.If(flagged(dve) > 0):
                    first_layer.vector(dve)
                    dve.wait_ge(first_layer.T["x_in"], 16)
                    with dve.Fori(0, NB) as b:
                        with first_layer.count.loop(b, NB, POST_STEPS):
                            for i in range(16):
                                nodes.vector(dve, i, b * TB, b + POSTS, agg[:, bass.ds(b * TB, TB), :],
                                             first_layer.count)
                    dve.nop()

        second_layer = Dense("dense_1", False)
        names = ("mask_ready", "product_ready", "first_rows", "shift_summed", "rows_done", "sum_ready",
                 "total_ready", "var_ready_bn", "std_bn", "leaky_ready", "out_ready", "last_out_ready",
                 "out_written")
        B = {k: sem(k) for k in names}
        ygathered = [sem(f"y_gathered_{i}") for i in range(2)]
        acc = wide_a[:, 0:2 * TB * D].rearrange("p (s t d) -> p s t d", s=2, d=D)
        shift = wide_a[:, 4 * TB * D:5 * TB * D].rearrange("p (t d) -> p t d", d=D)
        flat = lambda a: a.rearrange("p t d -> p (t d)")

        with nc.Block() as block:
            @block.gpsimd
            def _(pool):
                with pool.If(flagged(pool) < 1):
                    for b in range(NB):
                        if b >= 2:
                            pool.wait_ge(B["product_ready"], b - 1)
                        for q in range(PB):
                            column = columns[:, b * PB + q:b * PB + q + 1]
                            nc.gpsimd.indirect_dma_start(ygat[:, b % 2, q, :], None, ytable[:, :],
                                                         bass.IndirectOffsetOnAxis(column, 0))\
                                .then_inc(ygathered[b % 2], 16)
                    pool.nop()
                for c in range(NC - 1):
                    r = slice(c * CT, (c + 1) * CT)
                    pool.wait_ge(B["leaky_ready"], c + 1)
                    nc.gpsimd.tensor_tensor(xs[:, r, :], xs[:, r, :], agg[:, r, :], ALU.add)\
                        .then_inc(B["out_ready"], 1)

            @block.tensor
            def _(pe):
                def shift_sum():
                    pe.wait_ge(B["first_rows"], 1)
                    pe.matmul(slot_ps[:, 0:TB * D], ones, flat(agg[:, 0:TB, :]), start=True, stop=True)\
                        .then_inc(B["shift_summed"], 1)
                with pe.If(flagged(pe) > 0):
                    second_layer.tensor(pe)
                    shift_sum()
                    pe.nop()
                with pe.Else():
                    def product(b, odd, first=False):
                        pe.wait_ge(ygathered[odd], (b - odd) * (8 * PB) + 16 * PB)
                        pe.wait_ge(B["mask_ready"], b + 1)
                        if not first:
                            pe.wait_ge(B["rows_done"], b - 1)
                        for t in range(PB):
                            q, r = 32 * (t % 4), t // 4
                            ins = pe.matmul(work[q:q + 32, 512 * odd + r * D:512 * odd + (r + 1) * D],
                                            mstat[:, odd, t * 32:(t + 1) * 32], ygat[:, odd, t, :],
                                            start=True, stop=True, tile_position=(0, q))
                        ins.then_inc(B["product_ready"], 1)
                    product(0, 0, first=True)
                    shift_sum()
                    product(1, 1, first=True)
                    with pe.Fori(1, NB // 2) as k:
                        for odd in range(2):
                            product(2 * k + odd, odd)
                    pe.nop()
                pe.wait_ge(B["sum_ready"], 1)
                pe.matmul(work[:, 0:2 * TB * D], ones, wide_a[:, 0:2 * TB * D], start=True, stop=True)\
                    .then_inc(B["total_ready"], 1)

            @block.scalar
            def _(act):
                with act.If(flagged(act) > 0):
                    second_layer.scalar(act)
                    act.nop()
                with act.Else():
                    def mask_of(b, odd, first=False):
                        if not first:
                            act.wait_ge(B["product_ready"], b - 1)
                        act.activation(mstat[:, odd, :], mask[:, bass.ds(b * (PB * 32), PB * 32)], ACT.Copy)\
                            .then_inc(B["mask_ready"], 1)
                    mask_of(0, 0, first=True)
                    mask_of(1, 1, first=True)
                    with act.Fori(1, NB // 2) as k:
                        for odd in range(2):
                            mask_of(2 * k + odd, odd)
                    act.nop()
                act.wait_ge(B["var_ready_bn"], 1)
                act.activation(bn[:, 3, :], bn[:, 2, :], ACT.Sqrt).then_inc(B["std_bn"], 1)

            @block.vector
            def _(dve):
                then(V.memset(acc, 0.0))

                def rows_of(b, product, count, first=False):
                    rows = bass.ds(b * TB, TB)
                    then(V.tensor_tensor(pxc[:], product, ys[:, rows, :], ALU.add), count)
                    if first:
                        V.tensor_tensor(agg[:, rows, :], pxc[:], bc(dinv[:, rows], TB), ALU.mult)\
                            .then_inc(B["first_rows"], 1)
                        dve.wait_ge(B["first_rows"], 1)
                        then(V.tensor_copy(psq[:], agg[:, rows, :]), count)
                        dve.wait_ge(B["shift_summed"], 1)
                        then(V.tensor_copy(pnat[:], slot_ps[:, 0:TB * D].rearrange("p (t d) -> p t d", d=D)), count)
                        then(V.tensor_tensor(shift[:, 0, :], pnat[:, 0, :], pnat[:, 1, :], ALU.add), count)
                        then(V.tensor_scalar(shift[:, 0, :], shift[:, 0, :], 1.0 / (TB * P), None, ALU.mult), count)
                        then(V.tensor_copy(shift[:, 1, :], shift[:, 0, :]), count)
                    else:
                        then(V.tensor_tensor(psq[:], pxc[:], bc(dinv[:, rows], TB), ALU.mult), count)
                    V.tensor_tensor(agg[:, rows, :], psq[:], shift, ALU.subtract).then_inc(B["rows_done"], 1)
                    dve.wait_ge(B["rows_done"], b + 1)
                    V.tensor_tensor(acc[:, 0], acc[:, 0], agg[:, rows, :], ALU.add)
                    then(V.tensor_tensor(pxc[:], agg[:, rows, :], agg[:, rows, :], ALU.mult), count)
                    then(V.tensor_tensor(acc[:, 1], acc[:, 1], pxc[:], ALU.add), count)
                assert TB == 2
                with dve.If(flagged(dve) > 0):
                    second_layer.vector(dve)
                    rows_of(0, agg[:, 0:TB, :], second_layer.count, first=True)
                    with dve.Fori(1, NB) as b:
                        with second_layer.count.loop(b - 1, NB - 1, 4):
                            rows_of(b, agg[:, bass.ds(b * TB, TB), :], second_layer.count)
                    dve.nop()
                with dve.Else():
                    count = Count(sem("rows_step"))

                    def rows_from_product(b, odd, first=False):
                        dve.wait_ge(B["product_ready"], b + 1)
                        rows_of(b, work[:, 512 * odd:512 * odd + TB * D].rearrange("p (t d) -> p t d", d=D),
                                count, first)
                    rows_from_product(0, 0, first=True)
                    rows_from_product(1, 1)
                    with dve.Fori(0, NB // 2 - 1) as k:
                        with count.loop(k, NB // 2 - 1, 8):
                            for odd in range(2):
                                rows_from_product(2 * k + 2 + odd, odd)
                    dve.nop()
                V.memset(pst[:, 0, 0:1], 0.0).then_inc(B["sum_ready"], 1)
                dve.wait_ge(B["total_ready"], 1)
                then(V.tensor_reduce(bn[:, 0:2, :], work[:, 0:2 * TB * D].rearrange(
                    "p (s t d) -> p s d t", s=2, d=D), AX.X, ALU.add))
                then(V.tensor_scalar(bn[:, 0:2, :], bn[:, 0:2, :], 1.0 / N, None, ALU.mult))
                then(V.tensor_tensor(bn[:, 4, :], bn[:, 0, :], bn[:, 0, :], ALU.mult))
                then(V.tensor_tensor(bn[:, 5, :], bn[:, 1, :], bn[:, 4, :], ALU.subtract))
                V.tensor_scalar(bn[:, 2, :], bn[:, 5, :], 0.0, BN_EPS, ALU.max, ALU.add)\
                    .then_inc(B["var_ready_bn"], 1)
                dve.wait_ge(B["std_bn"], 1)
                factor, offset = bn[:, 4, :], bn[:, 5, :]
                then(V.reciprocal(bn[:, 1, :], bn[:, 3, :]))
                then(V.tensor_tensor(factor, bn[:, 1, :], par[:, 5:5 + D], ALU.mult))
                then(V.tensor_tensor(bn[:, 2, :], bn[:, 0, :], factor, ALU.mult))
                then(V.tensor_tensor(offset, par[:, 5 + D:5 + 2 * D], bn[:, 2, :], ALU.subtract))
                spread = lambda row: row.unsqueeze(1).to_broadcast([P, CT, D])
                for k in range(NC + 2):
                    if k >= 2:
                        a = agg[:, (k - 2) * CT:(k - 1) * CT, :]
                        ins = V.scalar_tensor_tensor(out=a, in0=a, scalar=SLOPE, in1=a, op0=ALU.mult, op1=ALU.max)
                        ins.then_inc(B["leaky_ready"], 1)
                    if 1 <= k <= NC:
                        a = agg[:, (k - 1) * CT:k * CT, :]
                        ins = V.tensor_tensor(a, a, spread(offset), ALU.add)
                        if k == NC:
                            then(ins)
                    if k < NC:
                        a = agg[:, k * CT:(k + 1) * CT, :]
                        then(V.tensor_tensor(a, a, spread(factor), ALU.mult))
                r = slice((NC - 1) * CT, NC * CT)
                dve.wait_ge(B["leaky_ready"], NC)
                V.tensor_tensor(xs[:, r, :], xs[:, r, :], agg[:, r, :], ALU.add).then_inc(B["last_out_ready"], 1)

            @block.sync
            def _(sp):
                with sp.If(flagged(sp) > 0):
                    second_layer.sync(sp)
                    sp.nop()
                for c in range(NC):
                    if c < NC - 1:
                        sp.wait_ge(B["out_ready"], c + 1)
                    else:
                        sp.wait_ge(B["last_out_ready"], 1)
                    sp.dma_start(out_t[:, c * CT:(c + 1) * CT, :], xs[:, c * CT:(c + 1) * CT, :])\
                        .then_inc(B["out_written"], 16)
                sp.wait_ge(B["out_written"], 16 * NC)


POST_STEPS = 13
DVE_STEPS = (30, 30, 0)

_INS = ["x", "adj", "L0_gnn_W", "L0_gnn_b", "L0_gnn_scale", "L0_gnn_Wq", "L0_gnn_bq", "L0_gnn_scale_q",
        "L0_gnn_Wk", "L0_gnn_bk", "L0_gnn_scale_k", "L0_gnn_att_bias", "L0_gnn_att_scale",
        "L1_gnn_W", "L1_gnn_b", "L1_gnn_gamma", "L1_gnn_beta"]


def kernel(**inputs):
    import numpy as np
    import concourse.bacc as bacc
    from concourse.bass_utils import run_bass_kernel_spmd

    nc = bacc.Bacc("TRN2", target_bir_lowering=False, num_devices=1)
    arrays, args = {}, []
    laid = {name: np.ascontiguousarray(inputs[name]) for name in _INS}
    for name, a in laid.items():
        if a.ndim == 0:
            laid[name] = a.reshape(1, 1)
    for name, a in {**laid, **host_constants(laid["x"].shape[0])}.items():
        arrays[f"in_{name}"] = a
        args.append(nc.dram_tensor(f"in_{name}", a.shape, mybir.dt.from_np(a.dtype), kind="ExternalInput").ap())
    out = nc.dram_tensor("out_0", laid["x"].shape, F32, kind="ExternalOutput").ap()
    graph_layers(nc, *args, out)
    r = run_bass_kernel_spmd(nc, [arrays], core_ids=[0])
    return r.results[0]["out_0"]
```
